# Optimizing a Trainium2 kernel written in Bass

```python
import numpy as np
import jax
import jax.numpy as jnp

def _softmax(x, axis=-1):
    return jax.nn.softmax(x, axis=axis)

def _gelu(x):
    return jax.nn.gelu(x, approximate=True)

def _silu(x):
    return jax.nn.silu(x)

def _sigmoid(x):
    return jax.nn.sigmoid(x)

def _layernorm(x, axis=-1, eps=1e-05):
    m = jnp.mean(x, axis=axis, keepdims=True)
    v = jnp.var(x, axis=axis, keepdims=True)
    return (x - m) / jnp.sqrt(v + eps)

def _scatter_add(tgt, idx, src, axis=0):
    return tgt.at[idx].add(src)

def _segment_sum(src, seg, n):
    return jax.ops.segment_sum(src, seg, n)
kernel_name = 'mk_sandwich_d1_jaxref_r8_239193'

def setup_inputs(seed: int=0):
    np.random.seed(seed)
    _w = jnp.asarray

    def _L0_attn_setup():
        import jax, jax.numpy as jnp
        import numpy as np
        B, T, D_MODEL, STATE = (4, 512, 128, 32)
        LN_EPS = 1e-05

        def _layernorm(x, w, b):
            mu = jnp.mean(x, axis=-1, keepdims=True)
            var = jnp.mean(jnp.square(x - mu), axis=-1, keepdims=True)
            return (x - mu) * jax.lax.rsqrt(var + LN_EPS) * w + b
        key = jax.random.key(seed)
        ks = jax.random.split(key, 8)
        x = jax.random.normal(ks[0], (B, T, D_MODEL), dtype=jnp.float32)
        bound_d = 1.0 / np.sqrt(D_MODEL)
        bound_n = 1.0 / np.sqrt(STATE)
        Wa_w = jax.random.normal(ks[1], (STATE, D_MODEL), dtype=jnp.float32) * 0.02
        Wa_b = jnp.zeros((STATE,), dtype=jnp.float32)
        WB_w = jax.random.normal(ks[2], (STATE, D_MODEL), dtype=jnp.float32) * 0.02
        WB_b = jax.random.uniform(ks[3], (STATE,), jnp.float32, -bound_d, bound_d)
        WC_w = jax.random.normal(ks[4], (D_MODEL, STATE), dtype=jnp.float32) * 0.02
        WC_b = jax.random.uniform(ks[5], (D_MODEL,), jnp.float32, -bound_n, bound_n)
        log_gamma = jnp.asarray(0.0, dtype=jnp.float32)
        D_skip = jax.random.normal(ks[6], (D_MODEL,), dtype=jnp.float32) * 0.01
        ln_w = jnp.ones((D_MODEL,), dtype=jnp.float32)
        ln_b = jnp.zeros((D_MODEL,), dtype=jnp.float32)
        return {'x': x, 'Wa_w': Wa_w, 'Wa_b': Wa_b, 'log_gamma': log_gamma, 'WB_w': WB_w, 'WB_b': WB_b, 'WC_w': WC_w, 'WC_b': WC_b, 'D_skip': D_skip, 'ln_w': ln_w, 'ln_b': ln_b}
    _L0_attn_in = _L0_attn_setup()

    def _L0_ffn_setup():
        import jax, jax.numpy as jnp
        import numpy as np
        B, S, D = (1, 256, 128)
        I = 256
        E = 8
        K = 2
        LIMIT = 7.0
        ALPHA = 1.702
        EPS = 1e-05

        def _swiglu(h):
            x_glu = jnp.minimum(h[..., ::2], LIMIT)
            x_lin = jnp.clip(h[..., 1::2], -LIMIT, LIMIT)
            return x_glu * jax.nn.sigmoid(ALPHA * x_glu) * (x_lin + 1.0)

        def _moe(t, gate_w, gate_b, mlp1_w, mlp1_b, mlp2_w, mlp2_b):
            T = t.shape[0]
            logits = t @ gate_w + gate_b
            top_v, top_i = jax.lax.top_k(logits, K)
            probs = jax.nn.softmax(top_v, axis=-1)
            w = jnp.zeros((T, E), t.dtype).at[jnp.arange(T)[:, None], top_i].set(probs)

            def body(acc, ew):
                w1, b1, w2, b2, we = ew
                h = _swiglu(t @ w1 + b1)
                y = h @ w2 + b2
                return (acc + we[:, None] * y, None)
            acc0 = jnp.zeros((T, t.shape[1]), t.dtype)
            acc, _ = jax.lax.scan(body, acc0, (mlp1_w, mlp1_b, mlp2_w, mlp2_b, w.T))
            return acc
        key = jax.random.key(seed)
        ks = jax.random.split(key, 4)
        s = 0.02
        return {'x': jax.random.normal(ks[0], (B, S, D), jnp.float32), 'norm_scale': jnp.ones((D,), jnp.float32), 'gate_w': jax.random.normal(ks[1], (D, E), jnp.float32) * s, 'gate_b': jnp.zeros((E,), jnp.float32), 'mlp1_w': jax.random.normal(ks[2], (E, D, 2 * I), jnp.float32) * s, 'mlp1_b': jnp.zeros((E, 2 * I), jnp.float32), 'mlp2_w': jax.random.normal(ks[3], (E, I, D), jnp.float32) * s, 'mlp2_b': jnp.zeros((E, D), jnp.float32)}
    _L0_ffn_in = _L0_ffn_setup()
    _d = {'L0_attn_x': _L0_attn_in['x'], 'L0_attn_Wa_w': _L0_attn_in['Wa_w'], 'L0_attn_Wa_b': _L0_attn_in['Wa_b'], 'L0_attn_log_gamma': _L0_attn_in['log_gamma'], 'L0_attn_WB_w': _L0_attn_in['WB_w'], 'L0_attn_WB_b': _L0_attn_in['WB_b'], 'L0_attn_WC_w': _L0_attn_in['WC_w'], 'L0_attn_WC_b': _L0_attn_in['WC_b'], 'L0_attn_D_skip': _L0_attn_in['D_skip'], 'L0_attn_ln_w': _L0_attn_in['ln_w'], 'L0_attn_ln_b': _L0_attn_in['ln_b'], 'L0_ffn_norm_scale': _L0_ffn_in['norm_scale'], 'L0_ffn_gate_w': _L0_ffn_in['gate_w'], 'L0_ffn_gate_b': _L0_ffn_in['gate_b'], 'L0_ffn_mlp1_w': _L0_ffn_in['mlp1_w'], 'L0_ffn_mlp1_b': _L0_ffn_in['mlp1_b'], 'L0_ffn_mlp2_w': _L0_ffn_in['mlp2_w'], 'L0_ffn_mlp2_b': _L0_ffn_in['mlp2_b']}
    _x0 = _d['L0_attn_x']
    _d['L0_attn_x'] = jax.random.normal(jax.random.fold_in(jax.random.key(seed), 1), (8, 512, 128), dtype=_x0.dtype)
    del _x0
    return _d

def reference(L0_attn_x, L0_attn_Wa_w, L0_attn_Wa_b, L0_attn_log_gamma, L0_attn_WB_w, L0_attn_WB_b, L0_attn_WC_w, L0_attn_WC_b, L0_attn_D_skip, L0_attn_ln_w, L0_attn_ln_b, L0_ffn_norm_scale, L0_ffn_gate_w, L0_ffn_gate_b, L0_ffn_mlp1_w, L0_ffn_mlp1_b, L0_ffn_mlp2_w, L0_ffn_mlp2_b):

    def _L0_attn_ref(x, Wa_w, Wa_b, log_gamma, WB_w, WB_b, WC_w, WC_b, D_skip, ln_w, ln_b):
        import jax, jax.numpy as jnp
        import numpy as np
        B, T, D_MODEL, STATE = (4, 512, 128, 32)
        LN_EPS = 1e-05

        def _layernorm(x, w, b):
            mu = jnp.mean(x, axis=-1, keepdims=True)
            var = jnp.mean(jnp.square(x - mu), axis=-1, keepdims=True)
            return (x - mu) * jax.lax.rsqrt(var + LN_EPS) * w + b
        residual = x
        xn = _layernorm(x, ln_w, ln_b)
        gamma = jax.nn.sigmoid(log_gamma)
        a = gamma * jnp.tanh(jnp.einsum('btd,nd->btn', xn, Wa_w) + Wa_b)
        a_hat = jnp.fft.fft(a, axis=-1)
        mag = jnp.maximum(jnp.abs(a_hat), 1e-08)
        a_hat = a_hat * jax.nn.sigmoid(2.0 * (1.0 - mag))
        u = jnp.einsum('btd,nd->btn', xn, WB_w) + WB_b
        u_hat = jnp.fft.fft(u, axis=-1)

        def combine(c1, c2):
            a1, b1 = c1
            a2, b2 = c2
            return (a1 * a2, a2 * b1 + b2)
        _, h_hat = jax.lax.associative_scan(combine, (a_hat, u_hat), axis=1)
        h = jnp.real(jnp.fft.ifft(h_hat, axis=-1)).astype(x.dtype)
        y = jnp.einsum('btn,dn->btd', h, WC_w) + WC_b + D_skip * residual
        return y

    def _L0_ffn_ref(x, norm_scale, gate_w, gate_b, mlp1_w, mlp1_b, mlp2_w, mlp2_b):
        import jax, jax.numpy as jnp
        import numpy as np
        B, S, D = (1, 256, 128)
        I = 256
        E = 8
        K = 2
        LIMIT = 7.0
        ALPHA = 1.702
        EPS = 1e-05

        def _swiglu(h):
            x_glu = jnp.minimum(h[..., ::2], LIMIT)
            x_lin = jnp.clip(h[..., 1::2], -LIMIT, LIMIT)
            return x_glu * jax.nn.sigmoid(ALPHA * x_glu) * (x_lin + 1.0)

        def _moe(t, gate_w, gate_b, mlp1_w, mlp1_b, mlp2_w, mlp2_b):
            T = t.shape[0]
            logits = t @ gate_w + gate_b
            top_v, top_i = jax.lax.top_k(logits, K)
            probs = jax.nn.softmax(top_v, axis=-1)
            w = jnp.zeros((T, E), t.dtype).at[jnp.arange(T)[:, None], top_i].set(probs)

            def body(acc, ew):
                w1, b1, w2, b2, we = ew
                h = _swiglu(t @ w1 + b1)
                y = h @ w2 + b2
                return (acc + we[:, None] * y, None)
            acc0 = jnp.zeros((T, t.shape[1]), t.dtype)
            acc, _ = jax.lax.scan(body, acc0, (mlp1_w, mlp1_b, mlp2_w, mlp2_b, w.T))
            return acc
        Bx, Sx, Dx = x.shape
        ms = jnp.mean(x * x, axis=-1, keepdims=True)
        t = (x * jax.lax.rsqrt(ms + EPS) * norm_scale).reshape(Bx * Sx, Dx)
        y = _moe(t, gate_w, gate_b, mlp1_w, mlp1_b, mlp2_w, mlp2_b)
        return x + y.reshape(Bx, Sx, Dx)
    x = L0_attn_x
    x = x + _layernorm(_L0_attn_ref(_layernorm(x, axis=-1), L0_attn_Wa_w, L0_attn_Wa_b, L0_attn_log_gamma, L0_attn_WB_w, L0_attn_WB_b, L0_attn_WC_w, L0_attn_WC_b, L0_attn_D_skip, L0_attn_ln_w, L0_attn_ln_b), axis=-1)
    x = x + _layernorm(_L0_ffn_ref(_layernorm(x, axis=-1), L0_ffn_norm_scale, L0_ffn_gate_w, L0_ffn_gate_b, L0_ffn_mlp1_w, L0_ffn_mlp1_b, L0_ffn_mlp2_w, L0_ffn_mlp2_b), axis=-1)
    return x

_drawn_inputs = setup_inputs


def setup_inputs(seed=0):
    import zlib

    import numpy as np

    out = dict(_drawn_inputs(seed))
    spreads = {'L0_attn_Wa_b': (0.0, 0.1),
     'L0_attn_ln_w': (1.0, 0.2),
     'L0_attn_ln_b': (0.0, 0.305),
     'L0_ffn_norm_scale': (1.0, 0.6),
     'L0_ffn_gate_b': (0.0, 0.347),
     'L0_ffn_mlp1_b': (0.0, 0.8),
     'L0_ffn_mlp2_b': (0.0, 0.269)}
    factors = {'L0_ffn_mlp1_w': 4.833, 'L0_ffn_mlp2_w': 4.487}
    for name, (base, spread) in spreads.items():
        noise = np.random.default_rng([zlib.crc32(name.encode()), seed]).standard_normal(out[name].shape)
        drawn = base * np.exp(spread * noise) if base else spread * noise
        out[name] = jnp.asarray(drawn.astype(out[name].dtype))
    for name, factor in factors.items():
        out[name] = (out[name] * factor).astype(out[name].dtype)
    return out
```

```python
from contextlib import ExitStack

import numpy as np
import concourse.bass as bass
from concourse import mybir

ALU = mybir.AluOpType
ACT = mybir.ActivationFunctionType
AX = mybir.AxisListType
F32 = mybir.dt.float32
F32R = mybir.dt.float32r
I32 = mybir.dt.int32

P = 128
B, T, D = 8, 512, 128
NS = 32
BG = 4
NG = B // BG
TT = T // P
NU = NG * TT
UT = BG * P
NE = 8
HB = 2
L = 8
C1 = T // L
C2 = C1 // L
KB = NS // 2 - 1
EPS = 1e-5
ALPHA = 1.702
LIMIT = 7.0
NBANK = 8


def shape_constants():
    dft = np.zeros((P, 2, NG, P))
    idft = np.zeros((P, 2, NG, P))
    n = np.arange(NS)
    for b in range(B):
        g, i = divmod(b, BG)
        rows = slice(i * NS, i * NS + NS)
        for plane, sign in ((0, np.ones(NS)), (1, (-1.0) ** n)):
            dft[rows, plane, g, b] = sign
            idft[b, plane, g, rows] = sign / NS
        for k in range(1, KB + 1):
            r = B + b * KB + k - 1
            cos, sin = np.cos(2 * np.pi * k * n / NS), np.sin(2 * np.pi * k * n / NS)
            dft[rows, 0, g, r], dft[rows, 1, g, r] = cos, -sin
            idft[r, 0, g, rows], idft[r, 1, g, rows] = 2 * cos / NS, -2 * sin / NS
    select = np.zeros((2 * NE, NE, P))
    for e in range(NE):
        select[e, e], select[e + NE, e] = 1.0, 1.0
    rank = np.tile(NE - np.arange(NE), (P, 1))
    return {"ident": np.eye(P), "dft": dft, "idft": idft, "select": select, "rank": rank}


def build(nc, x, wab, bab, log_gamma, wc4, rows2, cols3, gate_w, gate_b, w1, b1, w2, b2x2,
          ident, dft, idft, select, rank, out):
    with ExitStack() as ctx:
        def sb(name, shape, dt=F32):
            return ctx.enter_context(nc.sbuf_tensor(name, shape, dt))

        def sem(name):
            return ctx.enter_context(nc.semaphore(name))

        bank = ctx.enter_context(nc.psum_tensor("bank", [P, NBANK, 512], F32))

        X = sb("X", [P, NU, BG, D])
        R = sb("R", [P, NU, BG, D])
        Z = sb("Z", [P, 2, BG, D])
        xnT = sb("xnT", [P, 2, T])
        wab_s = sb("wab_s", [P, 2, BG, P])
        bab_s = sb("bab_s", [P, 2])
        gam = sb("gam", [P, 2])
        wc4_s = sb("wc4_s", [P, BG * D])
        rows_s = sb("rows_s", [P, 2, D])
        cols_s = sb("cols_s", [P, 3])
        gate_ws = sb("gate_ws", [P, NE])
        gate_bs = sb("gate_bs", [P, NE])
        rank_s = sb("rank_s", [P, NE])
        ident_s = sb("ident_s", [P, P])
        dft_s = sb("dft_s", [P, 2, NG, P])
        dftg = sb("dftg", [P, 2, NG, P])
        idft_s = sb("idft_s", [P, 2, NG, P])
        w1_st = sb("w1_st", [P, 2, 2 * HB * P])
        w1_hi = sb("w1_hi", [P, NE, 2, HB, P], F32R)
        w1_lo = sb("w1_lo", [P, NE, 2, HB, P], F32R)
        w2_s = sb("w2_s", [P, NE, HB, D])
        b1_s = sb("b1_s", [P, NE, 2, HB])
        b2_s = sb("b2_s", [2 * NE, D])
        b2_hi = sb("b2_hi", [2 * NE, D], F32R)
        b2_lo = sb("b2_lo", [2 * NE, D], F32R)
        sel_r = sb("sel_r", [2 * NE, NE, P], F32R)
        st = sb("st", [P, 2, BG, 6])
        mv = sb("mv", [P, 3, B, BG, 2])
        nrm = sb("nrm", [P, 3, B, 5, BG])
        half = sb("half", [P, 8])
        au = sb("au", [P, 2, NG, T])
        areal = wab_s[0:B, :, :, :].rearrange("p r i m -> p r (i m)")
        ureal = sb("ureal", [B, 2, T])
        hreal = xnT[0:B, :, :]
        acuc = sb("acuc", [P, 5, L, C1])
        acol, ucol = acuc[:, 0:3, :, :], acuc[:, 3:5, :, :]
        S = sb("S", [P, 4, L, C1])
        a2 = sb("a2", [P, 3, C1])
        S2 = sb("S2", [P, 4, C1])
        a3 = sb("a3", [P, 3, C2])
        S3 = sb("S3", [P, 2, C2])
        pr = sb("pr", [P, 2, 2, L * C1])
        sq, gt = pr[:, 0, :, :], pr[:, 1, 0, :]
        hT = sb("hT", [P, NG, T])
        sel_s = hT[0:2 * NE, :, :].rearrange("p a b -> p (a b)").rearrange("p (e m) -> p e m", m=P)
        tT = sb("tT", [P, 2, UT])
        tT_hi = sb("tT_hi", [P, NU * UT], F32R)
        tT_lo = sb("tT_lo", [P, NU * UT], F32R)
        NT = NU * BG
        TE = NT * NE
        w1_flat = w1_st[:].rearrange("p a b -> p (a b)")
        xn_flat = xnT[:].rearrange("p a b -> p (a b)")

        def router_view(flat, k, *shape):
            v = flat[:, k * TE:k * TE + int(np.prod(shape))]
            names = "abc"[:len(shape)]
            sizes = dict(zip(names, shape))
            return v.rearrange(f"p ({' '.join(names)}) -> p {' '.join(names)}", **sizes)

        lg = router_view(w1_flat, 0, 2, NT, NE)
        oh = router_view(w1_flat, 2, 2, NT, NE)
        eq = router_view(xn_flat, 0, NT, NE)
        wtok = router_view(xn_flat, 1, NT, NE)
        whl = router_view(xn_flat, 2, NT, 2 * NE)
        m12 = sb("m12", [P, 6, NT])
        whi = sb("whi", [P, NT, NE], F32R)
        wT = sb("wT", [2 * NE, NU * UT], F32R)
        gact = au
        lin = S[:].rearrange("p a l c -> p (a l c)").rearrange("p (b h t) -> p b h t", b=2, h=HB)
        prod = pr
        pw = acuc[:].rearrange("p a l c -> p (a l c)")[:, 0:2 * HB * UT]\
            .rearrange("p (b h t) -> p b h t", b=2, h=HB)
        wb = hT
        yT = Z[:, 0, :, :].rearrange("p i d -> p (i d)")
        O = tT[:, 0, :].rearrange("p (i d) -> p i d", d=D)
        fin = tT[:, 1, :].rearrange("p (i d) -> p i d", d=D)

        x_in = [sem(f"x_in{b}") for b in range(B)]
        small_in = sem("small_in")
        w1_in = [sem("w1_in0"), sem("w1_in1")]
        w1_split = sem("w1_split")
        w2_in = sem("w2_in")
        setup = sem("setup")
        gam_sig = sem("gam_sig")
        gam_scaled = sem("gam_scaled")
        half_set = sem("half_set")
        dve_chain = sem("dve_chain")
        pool_chain = sem("pool_chain")
        x_stats = sem("x_stats")
        x_scales = sem("x_scales")
        z_done = sem("z_done")
        zT_done = sem("zT_done")
        xn_done = sem("xn_done")
        proj_done = sem("proj_done")
        r0_done = sem("r0_done")
        skip_done = sem("skip_done")
        a_done = sem("a_done")
        u_done = sem("u_done")
        ahat_done = sem("ahat_done")
        uhat_done = sem("uhat_done")
        sq_done = sem("sq_done")
        mag2_done = sem("mag2_done")
        mag_done = sem("mag_done")
        guard_done = sem("guard_done")
        gate_done = sem("gate_done")
        ucol_done = sem("ucol_done")
        scan_done = sem("scan_done")
        ih_done = sem("ih_done")
        hT_done = sem("hT_done")
        y_done = sem("y_done")
        y_read = sem("y_read")
        y_stats = sem("y_stats")
        y_scales = sem("y_scales")
        yn_done = sem("yn_done")
        x1_done = sem("x1_done")
        x1_stats = sem("x1_stats")
        x1_scales = sem("x1_scales")
        t_done = sem("t_done")
        tTr_done = sem("tTr_done")
        tT_done = sem("tT_done")
        tT_split = sem("tT_split")
        r1_done = sem("r1_done")
        logit_done = sem("logit_done")
        gap_done = sem("gap_done")
        prob_done = sem("prob_done")
        whl_done = sem("whl_done")
        wTr_done = sem("wTr_done")
        wT_done = sem("wT_done")
        gl_ready = sem("gl_ready")
        w_ready = sem("w_ready")
        g_done = sem("g_done")
        l_done = sem("l_done")
        silu_done = sem("silu_done")
        wb_done = sem("wb_done")
        p_done = sem("p_done")
        pw_done = sem("pw_done")
        y2_done = sem("y2_done")
        yT_done = sem("yT_done")
        tr_done = sem("tr_done")
        clip_done = sem("clip_done")
        o_done = sem("o_done")
        o_bn = sem("o_bn")
        o_stats = sem("o_stats")
        o_scale = sem("o_scale")
        on_done = sem("on_done")
        fin_done = sem("fin_done")
        out_done = sem("out_done")

        block = ctx.enter_context(nc.Block())
        NSMALL = 15

        def zT_bank(n):
            return bank[:, n % 2, :]

        A_BANK, U_BANK, AHAT, UHAT, HT_BANK = 2, 4, 6, 0, 2
        Y_BANKS, LOGITS, WT_BANKS = 4, 2, (3, 4)
        Y2, WB, TR = 4, 5, 7

        def tile_of(b, j):
            return (b // BG) * TT + j, b % BG

        out_v = out.rearrange("(g i) (j p) d -> p g j i d", g=NG, p=P)

        @block.sync
        def _(sp):
            for b in range(B):
                g, i = divmod(b, BG)
                sp.dma_start(X[:, g * TT:(g + 1) * TT, i, :],
                             x[b].rearrange("(j p) d -> p j d", p=P)).then_inc(x_in[b], 16)
            for e in range(NE):
                if e >= 2:
                    sp.wait_ge(w1_split, e - 1)
                sp.dma_start(w1_st[:, e % 2, :], w1[:, e, :]).then_inc(w1_in[e % 2], 16)
            sp.dma_start(w2_s[:], w2).then_inc(w2_in, 16)

            def store(u):
                sp.wait_ge(fin_done, u + 1)
                sp.dma_start(out_v[:, u // TT, u % TT, :, :], fin[:]).then_inc(out_done, 16)

            for u in range(NU):
                store(u)
            sp.wait_ge(out_done, 16 * NU)

        @block.gpsimd
        def _(pool):
            chain = [0]

            def link(ins):
                chain[0] += 1
                ins.then_inc(pool_chain, 1)
                pool.wait_ge(pool_chain, chain[0])

            pool.memset(half[:], -0.5).then_inc(half_set, 1)
            pool.wait_ge(half_set, 1)

            def one_scale(which, n):
                v = nrm[:, which, n, :, :]
                link(pool.tensor_tensor(v[:, 1, :], v[:, 0, :], half[:, 0:BG], ALU.pow))

            def two_scales(which, n, done):
                v = nrm[:, which, n, :, :]
                m = mv[:, which, n, :, :]
                one_scale(which, n)
                link(pool.tensor_tensor(v[:, 2, :], m[:, :, 1], v[:, 1, :], ALU.mult))
                link(pool.tensor_tensor(v[:, 4, :], v[:, 2, :], v[:, 1, :], ALU.mult))
                link(pool.tensor_scalar(v[:, 2, :], v[:, 4, :], EPS, None, ALU.add))
                link(pool.tensor_tensor(v[:, 3, :], v[:, 2, :], half[:, 0:BG], ALU.pow))
                link(pool.tensor_tensor(v[:, 3, :], v[:, 3, :], v[:, 1, :], ALU.mult))
                link(pool.tensor_tensor(v[:, 2, :], m[:, :, 0], v[:, 1, :], ALU.mult))
                pool.tensor_scalar(v[:, 4, :], v[:, 2, :], -1.0, None, ALU.mult).then_inc(done, 1)

            def skip_term(b):
                g, i = divmod(b, BG)
                r = R[:, g * TT:(g + 1) * TT, i, :]
                pool.wait_ge(r0_done, TT * (b + 1))
                link(pool.tensor_tensor(r, r, rows_s[:, 0:1, :].to_broadcast([P, TT, D]), ALU.mult))
                pool.tensor_tensor(r, r, rows_s[:, 1:2, :].to_broadcast([P, TT, D]),
                                   ALU.add).then_inc(skip_done, 1)

            for b in range(B):
                pool.wait_ge(x_stats, b + 1)
                two_scales(0, b, x_scales)
                if b == 2:
                    pool.wait_ge(small_in, 16 * NSMALL)
                if b >= 2:
                    skip_term(b - 2)
            skip_term(B - 2)
            skip_term(B - 1)

            for n in range(NU + 2):
                if n < NU:
                    pool.wait_ge(y_stats, n + 1)
                    one_scale_ins = nrm[:, 1, n, :, :]
                    pool.tensor_tensor(one_scale_ins[:, 1, :], one_scale_ins[:, 0, :], half[:, 0:BG],
                                       ALU.pow).then_inc(y_scales, 1)
                if 1 <= n <= NU:
                    pool.wait_ge(yn_done, BG * n)
                    pool.tensor_tensor(X[:, n - 1, :, :], X[:, n - 1, :, :], R[:, n - 1, :, :],
                                       ALU.add).then_inc(x1_done, 1)
                if n >= 2:
                    pool.wait_ge(x1_stats, n - 1)
                    two_scales(2, n - 2, x1_scales)

            def weigh(s, e):
                pool.wait_ge(p_done, s + 1)
                pool.wait_ge(wb_done, s + 1)
                pool.tensor_tensor(pw[:, e % 2, :, :], prod[:, e % 2, :, :],
                                   wb[:, e % 2:e % 2 + 1, :].to_broadcast([P, HB, UT]),
                                   ALU.mult).then_inc(pw_done, 1)

            def out_scale(v):
                pool.wait_ge(o_stats, v + 1)
                pool.tensor_tensor(nrm[:, 0, 0, 1, :], nrm[:, 0, 0, 0, :], half[:, 0:BG],
                                   ALU.pow).then_inc(o_scale, 1)

            def out_add(v):
                pool.wait_ge(on_done, BG * (v + 1))
                if not isinstance(v, int) or v >= 1:
                    pool.wait_ge(out_done, 16 * v)
                pool.tensor_tensor(fin[:], O[:], X[:, bass.ds(v, 1), :, :].rearrange("p a i d -> p (a i) d"),
                                   ALU.add).then_inc(fin_done, 1)

            def group(u, first):
                for e in range(NE):
                    s = u * NE + e
                    if not (first and e < 2):
                        pool.wait_ge(y2_done, s - 1)
                    weigh(s, e)
                    if not first and e == 2:
                        out_scale(u - 1)
                    if not first and e == 3:
                        out_add(u - 1)

            group(0, True)
            with pool.Fori(1, NU) as u:
                group(u, False)
            out_scale(NU - 1)
            out_add(NU - 1)

        @block.scalar
        def _(act):
            loads = [(ident_s[:], ident), (wab_s[:], wab), (bab_s[:], bab), (cols_s[:], cols3),
                     (gam[:, 0:1], log_gamma.to_broadcast([P, 1])), (dft_s[:], dft),
                     (rows_s[:], rows2.rearrange("(o r) d -> o r d", o=1).to_broadcast([P, 2, D])),
                     (idft_s[:], idft), (wc4_s[:], wc4), (gate_ws[:], gate_w),
                     (gate_bs[:], gate_b.to_broadcast([P, NE])),
                     (rank_s[:], rank), (b1_s[:], b1), (b2_s[:], b2x2), (sel_s[:], select)]
            assert len(loads) == NSMALL
            for dst, src in loads:
                act.dma_start(dst, src).then_inc(small_in, 16)
            act.wait_ge(small_in, 16 * NSMALL)
            act.activation(gam[:, 1:2], gam[:, 0:1], ACT.Sigmoid).then_inc(gam_sig, 1)

            def normal_x(b):
                for j in range(TT):
                    u, i = tile_of(b, j)
                    if j == 0:
                        act.wait_ge(x_scales, b + 1)
                    act.activation(R[:, u, i, :], X[:, u, i, :], ACT.Identity,
                                   bias=nrm[:, 0, b, 4, j:j + 1],
                                   scale=nrm[:, 0, b, 1, j:j + 1]).then_inc(r0_done, 1)

            def turn_x(b):
                act.wait_ge(zT_done, b + 1)
                if b >= 2:
                    act.wait_ge(proj_done, b - 1)
                act.activation(xnT[:, b % 2, :], zT_bank(b), ACT.Identity, bias=cols_s[:, 1:2],
                               scale=cols_s[:, 0:1]).then_inc(xn_done, 1)

            for b in range(B + 1):
                if b < B:
                    normal_x(b)
                if b >= 1:
                    turn_x(b - 1)
                if b in (BG + 1, B):
                    g = 0 if b == BG + 1 else 1
                    act.wait_ge(proj_done, BG * (g + 1))
                    act.activation(au[:, 0, g, :], bank[:, A_BANK + g, :], ACT.Tanh,
                                   bias=bab_s[:, 0:1]).then_inc(a_done, 1)
                    act.activation(au[:, 1, g, :], bank[:, U_BANK + g, :], ACT.Identity,
                                   bias=bab_s[:, 1:2]).then_inc(u_done, 1)

            act.wait_ge(ahat_done, 1)
            act.activation(sq[:], bank[:, AHAT:AHAT + 2, :], ACT.Square).then_inc(sq_done, 1)
            act.activation(areal[:], bank[0:B, AHAT:AHAT + 2, :], ACT.Abs).then_inc(sq_done, 1)
            act.wait_ge(uhat_done, 1)
            act.activation(ucol[:], bank[:, UHAT:UHAT + 2, :].rearrange("p r (c l) -> p r l c", l=L),
                           ACT.Identity).then_inc(ucol_done, 1)
            act.activation(ureal[:], bank[0:B, UHAT:UHAT + 2, :], ACT.Identity).then_inc(ucol_done, 1)
            act.wait_ge(mag2_done, 1)
            act.activation(gt[:], gt[:], ACT.Sqrt).then_inc(mag_done, 1)
            act.wait_ge(guard_done, 2)
            act.activation(gt[:], gt[:], ACT.Sigmoid, bias=2.0, scale=-2.0).then_inc(gate_done, 1)
            act.activation(areal[:], areal[:], ACT.Sigmoid, bias=2.0, scale=-2.0).then_inc(gate_done, 1)

            for g in range(NG):
                act.wait_ge(ih_done, g + 1)
                act.activation(hT[:, g, :].rearrange("p (c l) -> p l c", l=L),
                               bank[:, HT_BANK + g, :].rearrange("p (l c) -> p l c", l=L),
                               ACT.Identity).then_inc(hT_done, 1)

            for n in range(NU + 1):
                if n < NU:
                    act.wait_ge(x1_scales, n + 1)
                    for i in range(BG):
                        act.activation(R[:, n, i, :], X[:, n, i, :], ACT.Identity,
                                       bias=nrm[:, 2, n, 4, i:i + 1],
                                       scale=nrm[:, 2, n, 1, i:i + 1]).then_inc(r1_done, 1)
                if n >= 1:
                    m = n - 1
                    act.wait_ge(tTr_done, m + 1)
                    if m >= 2:
                        act.wait_ge(tT_split, m - 1)
                        act.wait_ge(logit_done, m - 1)
                    act.activation(tT[:, m % 2, :], zT_bank(m), ACT.Identity,
                                   scale=cols_s[:, 2:3]).then_inc(tT_done, 1)

            act.wait_ge(gap_done, 2)
            act.activation(m12[:, 4:6, :], m12[:, 2:4, :], ACT.Sigmoid).then_inc(prob_done, 1)
            for n in range(NU):
                act.wait_ge(wTr_done, n + 1)
                act.activation(wT[:, n * UT:(n + 1) * UT], bank[0:2 * NE, WT_BANKS[n % 2], :],
                               ACT.Identity).then_inc(wT_done, 1)

            def linear_half(s, e, h, first):
                k = s * 2 + h
                act.wait_ge(gl_ready, k + 1)
                if h == 0 and not (first and e < 2):
                    act.wait_ge(p_done, s - 1)
                act.activation(lin[:, e % 2, h, :], bank[:, 2 * h + 1, :], ACT.Identity,
                               bias=b1_s[:, e, 1, h:h + 1]).then_inc(l_done, 1)

            def group(u, first):
                for e in range(NE):
                    s = u * NE + e
                    act.wait_ge(w_ready, s + 1)
                    if not (first and e < 2):
                        act.wait_ge(pw_done, s - 1)
                    act.activation(wb[:, e % 2, :], bank[:, WB + e % 2, :], ACT.Copy,
                                   scale=1.0 / ALPHA).then_inc(wb_done, 1)
                    linear_half(s, e, 0, first)
                    linear_half(s, e, 1, first)
                    act.wait_ge(g_done, s * 2 + 2)
                    act.activation(gact[:, e % 2, :, :], gact[:, e % 2, :, :], ACT.Silu,
                                   scale=ALPHA).then_inc(silu_done, 1)
                    if e == 1 and not first:
                        evacuate_y(u - 1)

            def evacuate_y(v):
                act.wait_ge(y2_done, (v + 1) * NE)
                if not isinstance(v, int) or v >= 1:
                    act.wait_ge(tr_done, v)
                act.activation(yT[:], bank[:, Y2, :], ACT.Identity).then_inc(yT_done, 1)

            group(0, True)
            with act.Fori(1, NU) as u:
                group(u, False)
            evacuate_y(NU - 1)

        @block.vector
        def _(dve):
            chain = [0]

            def link(ins):
                chain[0] += 1
                ins.then_inc(dve_chain, 1)
                dve.wait_ge(dve_chain, chain[0])

            def loose(ins):
                chain[0] += 1
                ins.then_inc(dve_chain, 1)
                return chain[0]

            def stats(tiles, which, n, done):
                last = [loose(dve.bn_stats(st[:, n % 2, k, :], tl)) for k, tl in enumerate(tiles)]
                for k in range(BG):
                    dve.wait_ge(dve_chain, last[k])
                    end = loose(dve.bn_aggr(mv[:, which, n, k, :], st[:, n % 2, k, :]))
                dve.wait_ge(dve_chain, end)
                dve.tensor_scalar(nrm[:, which, n, 0, :], mv[:, which, n, :, 1], EPS, None,
                                  ALU.add).then_inc(done, 1)

            def scaled(dst, src, which, n, k, col, done):
                dve.tensor_scalar(dst, src, mv[:, which, n, k, 0:1], nrm[:, which, n, col, k:k + 1],
                                  ALU.subtract, ALU.mult).then_inc(done, 1)

            for b in range(B + 1):
                if b < B:
                    dve.wait_ge(x_in[b], 16)
                    stats([X[:, tile_of(b, j)[0], b % BG, :] for j in range(TT)], 0, b, x_stats)
                if b >= 1:
                    a = b - 1
                    dve.wait_ge(x_scales, a + 1)
                    if a >= 2:
                        dve.wait_ge(zT_done, a - 1)
                    for j in range(TT):
                        scaled(Z[:, a % 2, j, :], X[:, tile_of(a, j)[0], a % BG, :], 0, a, j, 3, z_done)
            dve.wait_ge(gam_sig, 1)
            dve.tensor_scalar(dftg[:], dft_s[:], gam[:, 1:2], None, ALU.mult).then_inc(gam_scaled, 1)
            for e in range(NE):
                dve.wait_ge(w1_in[e % 2], 16 * (e // 2 + 1))
                wv = w1_st[:, e % 2, :]
                hi = w1_hi[:, e, :, :, :].rearrange("p a b c -> p (a b c)")
                lo = w1_lo[:, e, :, :, :].rearrange("p a b c -> p (a b c)")
                link(dve.tensor_copy(hi, wv))
                dve.tensor_tensor(lo, wv, hi.bitcast(F32), ALU.subtract).then_inc(w1_split, 1)
            dve.wait_ge(small_in, 16 * NSMALL)
            dve.tensor_scalar(b1_s[:, :, 1, :], b1_s[:, :, 1, :], 1.0, None, ALU.add).then_inc(setup, 1)
            dve.tensor_copy(sel_r[:], sel_s[:]).then_inc(setup, 1)
            link(dve.tensor_copy(b2_hi[:], b2_s[:]))
            dve.tensor_tensor(b2_lo[:], b2_s[:], b2_hi[:].bitcast(F32), ALU.subtract).then_inc(setup, 1)

            dve.wait_ge(sq_done, 2)
            dve.tensor_tensor(gt[:], sq[:, 0, :], sq[:, 1, :], ALU.add).then_inc(mag2_done, 1)
            dve.tensor_scalar(areal[:], areal[:], 1e-8, None, ALU.max).then_inc(guard_done, 1)
            dve.wait_ge(mag_done, 1)
            dve.tensor_scalar(gt[:], gt[:], 1e-8, None, ALU.max).then_inc(guard_done, 1)
            dve.wait_ge(gate_done, 2)

            def chunked(ap):
                return ap.rearrange("p (c l) -> p l c", l=L)

            are, aim = bank[:, AHAT, :], bank[:, AHAT + 1, :]
            loose(dve.tensor_tensor(acol[:, 0, :, :], chunked(are), chunked(gt[:]), ALU.mult))
            loose(dve.tensor_tensor(acol[:, 2, :, :], chunked(aim), chunked(gt[:]), ALU.mult))
            link(dve.tensor_tensor(areal[:], bank[0:B, AHAT:AHAT + 2, :], areal[:], ALU.mult))
            dve.tensor_scalar(acol[:, 1, :, :], acol[:, 2, :, :], -1.0, None, ALU.mult)\
               .then_inc(dve_chain, 1)
            chain[0] += 1
            dve.wait_ge(ucol_done, 2)
            for r in range(2):
                end = loose(dve.tensor_tensor_scan(hreal[:, r, :], areal[:, r, :], ureal[:, r, :], 0.0,
                                                   ALU.mult, ALU.add))

            def scan_level(a, u, s, steps, width, planes):
                ks = planes // 2
                loose(dve.tensor_copy(s(0)[:, 0:2, :], u(0)))
                if ks == 2:
                    loose(dve.tensor_copy(s(0)[:, 2:3, :], a(0)[:, 0:1, :]))
                    loose(dve.tensor_copy(s(0)[:, 3:4, :], a(0)[:, 2:3, :]))
                for l in range(1, steps):
                    p1 = pr[:, 0, :, :].rearrange("p a b -> p (a b)")[:, 0:planes * width]
                    p2 = pr[:, 1, :, :].rearrange("p a b -> p (a b)")[:, 0:planes * width]
                    v1 = p1.rearrange("p (k w) -> p k w", k=planes)
                    v2 = p2.rearrange("p (k w) -> p k w", k=planes)
                    dve.wait_ge(dve_chain, chain[0])
                    loose(dve.tensor_tensor(v1, a(l)[:, 0:1, :].to_broadcast([P, planes, width]),
                                            s(l - 1), ALU.mult))
                    for j in range(2):
                        end = loose(dve.tensor_tensor(
                            v2[:, j:planes:2, :], a(l)[:, 1 + j:2 + j, :].to_broadcast([P, ks, width]),
                            s(l - 1)[:, 1 - j:planes:2, :], ALU.mult))
                    dve.wait_ge(dve_chain, end - 2)
                    loose(dve.tensor_tensor(v1[:, 0:2, :], v1[:, 0:2, :], u(l), ALU.add))
                    dve.wait_ge(dve_chain, chain[0])
                    loose(dve.tensor_tensor(s(l), v1, v2, ALU.add))
                dve.wait_ge(dve_chain, chain[0])

            def carry_level(s, carry, groups, width):
                n = groups * width
                p1 = pr[:, 0, :, 0:n].rearrange("p r (l c) -> p r l c", l=groups)
                p2 = pr[:, 1, :, 0:n].rearrange("p r (l c) -> p r l c", l=groups)
                for r in range(2):
                    bc = carry[:, r:r + 1, :].to_broadcast([P, groups, width])
                    loose(dve.tensor_tensor(p1[:, r, :, :], s[:, 2, :, :], bc, ALU.mult))
                    loose(dve.tensor_tensor(p2[:, r, :, :], s[:, 3, :, :], bc, ALU.mult))
                dve.wait_ge(dve_chain, chain[0] - 2)
                loose(dve.tensor_tensor(p1[:, 0, :, :], p1[:, 0, :, :], s[:, 0, :, :], ALU.add))
                dve.wait_ge(dve_chain, chain[0] - 1)
                loose(dve.tensor_tensor(p1[:, 1, :, :], p1[:, 1, :, :], s[:, 1, :, :], ALU.add))
                dve.wait_ge(dve_chain, chain[0] - 1)
                loose(dve.tensor_tensor(s[:, 0, :, :], p1[:, 0, :, :], p2[:, 1, :, :], ALU.subtract))
                dve.wait_ge(dve_chain, chain[0] - 1)
                loose(dve.tensor_tensor(s[:, 1, :, :], p1[:, 1, :, :], p2[:, 0, :, :], ALU.add))
                dve.wait_ge(dve_chain, chain[0])

            def ends(s, a):
                loose(dve.tensor_copy(a[:, 0:1, :], s[:, 2:3, :]))
                loose(dve.tensor_scalar(a[:, 1:2, :], s[:, 3:4, :], -1.0, None, ALU.mult))
                loose(dve.tensor_copy(a[:, 2:3, :], s[:, 3:4, :]))
                dve.wait_ge(dve_chain, chain[0])

            scan_level(lambda l: acol[:, :, l, :], lambda l: ucol[:, :, l, :], lambda l: S[:, :, l, :],
                       L, C1, 4)
            ends(S[:, :, L - 1, :], a2)
            end2 = S[:, :, L - 1, :]
            scan_level(lambda l: a2[:, :, l::L], lambda l: end2[:, 0:2, l::L], lambda l: S2[:, :, l::L],
                       L, C2, 4)
            ends(S2[:, :, L - 1::L], a3)
            end3 = S2[:, :, L - 1::L]
            scan_level(lambda l: a3[:, :, l:l + 1], lambda l: end3[:, 0:2, l:l + 1],
                       lambda l: S3[:, :, l:l + 1], C2, 1, 2)
            v2 = S2[:].rearrange("p r (c l) -> p r l c", l=L)
            carry_level(v2[:, :, :, 1:], S3[:, :, 0:C2 - 1], L, C2 - 1)
            carry_level(S[:, :, :, 1:], S2[:, 0:2, 0:C1 - 1], L, C1 - 1)
            dve.tensor_copy(S[0:B, 0:2, :, :], hreal[:].rearrange("p r (c l) -> p r l c", l=L))\
               .then_inc(scan_done, 1)

            def y_in(n):
                dve.wait_ge(y_done, n + 1)
                dve.wait_ge(skip_done, BG * (n // TT + 1))
                dve.tensor_tensor(R[:, n, :, :], bank[:, Y_BANKS + n % 4, :].rearrange("p (i d) -> p i d", d=D),
                                  R[:, n, :, :], ALU.add).then_inc(y_read, 1)
                dve.wait_ge(y_read, n + 1)
                stats([R[:, n, i, :] for i in range(BG)], 1, n, y_stats)

            def y_norm(n):
                dve.wait_ge(y_scales, n + 1)
                for i in range(BG):
                    scaled(R[:, n, i, :], R[:, n, i, :], 1, n, i, 1, yn_done)

            def x1_stat(n):
                dve.wait_ge(x1_done, n + 1)
                stats([X[:, n, i, :] for i in range(BG)], 2, n, x1_stats)

            def t_norm(n):
                dve.wait_ge(x1_scales, n + 1)
                dve.wait_ge(zT_done, B)
                if n >= 2:
                    dve.wait_ge(tTr_done, n - 1)
                for i in range(BG):
                    scaled(Z[:, n % 2, i, :], X[:, n, i, :], 2, n, i, 3, t_done)

            def t_split(n):
                dve.wait_ge(tT_done, n + 1)
                hi, lo = tT_hi[:, n * UT:(n + 1) * UT], tT_lo[:, n * UT:(n + 1) * UT]
                link(dve.tensor_copy(hi, tT[:, n % 2, :]))
                dve.tensor_tensor(lo, tT[:, n % 2, :], hi.bitcast(F32), ALU.subtract).then_inc(tT_split, 1)

            for n in range(NU + 4):
                for lag, stage in enumerate((y_in, y_norm, x1_stat, t_norm, t_split)):
                    if 0 <= n - lag < NU:
                        stage(n - lag)

            dve.wait_ge(logit_done, NU)

            def bc8(v):
                return v.rearrange("p (t o) -> p t o", o=1).to_broadcast([P, NT, NE])

            def bct(v):
                return v.rearrange("p (o e) -> p o e", o=1).to_broadcast([P, NT, NE])

            link(dve.tensor_tensor(lg[:, 0, :, :],
                                   bank[:, LOGITS, 0:NT * NE].rearrange("p (t e) -> p t e", e=NE),
                                   bct(gate_bs[:]), ALU.add))
            for k in range(2):
                link(dve.tensor_reduce(m12[:, k, :], lg[:, k, :, :], AX.X, ALU.max))
                link(dve.tensor_tensor(eq[:], lg[:, k, :, :], bc8(m12[:, k, :]), ALU.is_equal))
                link(dve.tensor_tensor(eq[:], eq[:], bct(rank_s[:]), ALU.mult))
                link(dve.tensor_reduce(m12[:, 4, :], eq[:], AX.X, ALU.max))
                link(dve.tensor_tensor(oh[:, k, :, :], bct(rank_s[:]), bc8(m12[:, 4, :]), ALU.is_equal))
                if k == 0:
                    flat = "p t e -> p (t e)"
                    link(dve.scalar_tensor_tensor(lg[:, 1, :, :].rearrange(flat),
                                                  oh[:, 0, :, :].rearrange(flat), -3.0e38,
                                                  lg[:, 0, :, :].rearrange(flat), ALU.mult, ALU.add))
            dve.tensor_tensor(m12[:, 2, :], m12[:, 0, :], m12[:, 1, :], ALU.subtract).then_inc(gap_done, 1)
            dve.tensor_tensor(m12[:, 3, :], m12[:, 1, :], m12[:, 0, :], ALU.subtract).then_inc(gap_done, 1)
            dve.wait_ge(prob_done, 1)
            link(dve.tensor_tensor(wtok[:], oh[:, 0, :, :], bc8(m12[:, 4, :]), ALU.mult))
            link(dve.tensor_tensor(eq[:], oh[:, 1, :, :], bc8(m12[:, 5, :]), ALU.mult))
            link(dve.tensor_tensor(wtok[:], wtok[:], eq[:], ALU.add))
            link(dve.tensor_copy(whi[:], wtok[:]))
            dve.tensor_copy(whl[:, :, 0:NE], whi[:].bitcast(F32)).then_inc(whl_done, 1)
            dve.tensor_tensor(whl[:, :, NE:2 * NE], wtok[:], whi[:].bitcast(F32),
                              ALU.subtract).then_inc(whl_done, 1)

            def glu_half(s, e, h, reused):
                if reused and h == 0:
                    dve.wait_ge(p_done, s - 1)
                dve.wait_ge(gl_ready, s * 2 + h + 1)
                dve.tensor_scalar(gact[:, e % 2, h, :], bank[:, 2 * h, :], b1_s[:, e, 0, h:h + 1],
                                  LIMIT, ALU.add, ALU.min).then_inc(g_done, 1)

            def clip(s, e):
                dve.wait_ge(l_done, s * 2 + 2)
                dve.tensor_scalar(lin[:, e % 2, :, :], lin[:, e % 2, :, :], LIMIT + 1.0, 1.0 - LIMIT,
                                  ALU.min, ALU.max).then_inc(clip_done, 1)

            def combine(s, e, reused):
                dve.wait_ge(clip_done, s + 1)
                dve.wait_ge(silu_done, s + 1)
                if reused:
                    dve.wait_ge(pw_done, s - 1)
                dve.tensor_tensor(prod[:, e % 2, :, :], lin[:, e % 2, :, :], gact[:, e % 2, :, :],
                                  ALU.mult).then_inc(p_done, 1)

            def out_in(v):
                dve.wait_ge(tr_done, v + 1)
                if not isinstance(v, int) or v >= 1:
                    dve.wait_ge(fin_done, v)
                dve.tensor_tensor(O[:], bank[:, TR, :].rearrange("p (i d) -> p i d", d=D),
                                  R[:, bass.ds(v, 1), :, :].rearrange("p a i d -> p (a i) d"),
                                  ALU.add).then_inc(o_done, 1)
                dve.wait_ge(o_done, v + 1)
                for i in range(BG):
                    dve.bn_stats(st[:, 0, i, :], O[:, i, :]).then_inc(o_bn, 1)

            def out_aggregate(v):
                for i in range(BG):
                    dve.bn_aggr(mv[:, 0, 0, i, :], st[:, 0, i, :]).then_inc(o_bn, 1)
                dve.wait_ge(o_bn, (v + 1) * 2 * BG)
                dve.tensor_scalar(nrm[:, 0, 0, 0, :], mv[:, 0, 0, :, 1], EPS, None,
                                  ALU.add).then_inc(o_stats, 1)

            def out_norm(v):
                dve.wait_ge(o_scale, v + 1)
                for i in range(BG):
                    scaled(O[:, i, :], O[:, i, :], 0, 0, i, 1, on_done)

            def group(u, first):
                for e in range(NE):
                    s = u * NE + e
                    if not first and e == 3:
                        dve.wait_ge(o_bn, (u - 1) * 2 * BG + BG)
                    if not (first and e == 0):
                        clip(s - 1, (e - 1) % NE)
                    glu_half(s, e, 0, not (first and e < 2))
                    if not (first and e == 0):
                        combine(s - 1, (e - 1) % NE, not (first and e < 3))
                    glu_half(s, e, 1, True)
                    if not first and e == 2:
                        out_in(u - 1)
                    if not first and e == 3:
                        out_aggregate(u - 1)
                    if not first and e == 4:
                        out_norm(u - 1)

            group(0, True)
            with dve.Fori(1, NU) as u:
                group(u, False)
            clip(NU * NE - 1, NE - 1)
            combine(NU * NE - 1, NE - 1, True)
            out_in(NU - 1)
            dve.wait_ge(o_bn, (NU - 1) * 2 * BG + BG)
            out_aggregate(NU - 1)
            out_norm(NU - 1)

        @block.tensor
        def _(pe):
            pe.wait_ge(small_in, 16 * NSMALL)

            def turn_four(dst, src, done):
                for i in range(BG):
                    last = pe.transpose(dst[:, i * P:(i + 1) * P], src(i), ident_s[:])
                last.then_inc(done, 1)

            for b in range(B + 1):
                if b < B:
                    pe.wait_ge(z_done, TT * (b + 1))
                    if b >= 2:
                        pe.wait_ge(xn_done, b - 1)
                    turn_four(zT_bank(b), lambda i: Z[:, b % 2, i, :], zT_done)
                if b >= 1:
                    g, i = divmod(b - 1, BG)
                    pe.wait_ge(xn_done, b)
                    for r, to in ((0, A_BANK), (1, U_BANK)):
                        last = pe.matmul(bank[:, to + g, :], wab_s[:, r, i, :], xnT[:, (b - 1) % 2, :],
                                         start=(i == 0), stop=(i == BG - 1))
                    last.then_inc(proj_done, 1)

            pe.wait_ge(gam_scaled, 1)
            for r in range(2):
                for g in range(NG):
                    pe.wait_ge(a_done, g + 1)
                    last = pe.matmul(bank[:, AHAT + r, :], dftg[:, r, g, :], au[:, 0, g, :],
                                     start=(g == 0), stop=(g == NG - 1))
            last.then_inc(ahat_done, 1)
            pe.wait_ge(u_done, NG)
            pe.wait_ge(xn_done, B)
            for r in range(2):
                for g in range(NG):
                    last = pe.matmul(bank[:, UHAT + r, :], dft_s[:, r, g, :], au[:, 1, g, :],
                                     start=(g == 0), stop=(g == NG - 1))
            last.then_inc(uhat_done, 1)

            pe.wait_ge(scan_done, 1)
            for g in range(NG):
                for r in range(2):
                    last = pe.matmul(bank[:, HT_BANK + g, :], idft_s[:, r, g, :],
                                     S[:, r, :, :].rearrange("p l c -> p (l c)"),
                                     start=(r == 0), stop=(r == 1))
                last.then_inc(ih_done, 1)

            def project(n):
                g, j = divmod(n, TT)
                pe.wait_ge(hT_done, g + 1)
                if n >= 4:
                    pe.wait_ge(y_read, n - 3)
                pe.matmul(bank[:, Y_BANKS + n % 4, :], hT[:, g, j * P:(j + 1) * P], wc4_s[:],
                          start=True, stop=True).then_inc(y_done, 1)

            def turn_t(n):
                pe.wait_ge(t_done, BG * (n + 1))
                pe.wait_ge(ucol_done, 2)
                if n >= 2:
                    pe.wait_ge(tT_done, n - 1)
                turn_four(zT_bank(n), lambda i: Z[:, n % 2, i, :], tTr_done)

            def logits(n):
                pe.wait_ge(tT_done, n + 1)
                pe.wait_ge(hT_done, NG)
                for i in range(BG):
                    t = n * BG + i
                    last = pe.matmul(bank[:, LOGITS, t * NE:(t + 1) * NE], tT[:, n % 2, i * P:(i + 1) * P],
                                     gate_ws[:], start=True, stop=True)
                last.then_inc(logit_done, 1)

            for n in range(4):
                project(n)
            for n in range(NU + 1):
                if n + 4 < NU:
                    project(n + 4)
                if n < NU:
                    turn_t(n)
                if n >= 1:
                    logits(n - 1)

            pe.wait_ge(whl_done, 2)
            pe.wait_ge(y_read, NU)
            for n in range(NU):
                if n >= 2:
                    pe.wait_ge(wT_done, n - 1)
                for i in range(BG):
                    last = pe.transpose(bank[0:2 * NE, WT_BANKS[n % 2], i * P:(i + 1) * P],
                                        whl[:, n * BG + i, :], ident_s[:])
                last.then_inc(wTr_done, 1)

            def weights_out(u, e):
                pe.matmul(bank[:, WB + e % 2, :], sel_r[:, e, :], wT[:, bass.ds(u * UT, UT)],
                          start=True, stop=True).then_inc(w_ready, 1)

            def mlp1_half(u, s, e, h, first):
                k = s * 2 + h
                if not (first and e == 0):
                    pe.wait_ge(g_done, k - 1)
                    pe.wait_ge(l_done, k - 1)
                hi, lo = tT_hi[:, bass.ds(u * UT, UT)], tT_lo[:, bass.ds(u * UT, UT)]
                for r in range(2):
                    dst = bank[:, 2 * h + r, :]
                    pe.matmul(dst, w1_hi[:, e, r, h, :], hi, start=True, stop=False)
                    pe.matmul(dst, w1_hi[:, e, r, h, :], lo, start=False, stop=False)
                    last = pe.matmul(dst, w1_lo[:, e, r, h, :], hi, start=False, stop=True)
                last.then_inc(gl_ready, 1)

            def mlp2(u, s, e, first):
                if e == 0 and not first:
                    pe.wait_ge(yT_done, u)
                pe.wait_ge(pw_done, s + 1)
                for h in range(HB):
                    last = pe.matmul(bank[:, Y2, :], w2_s[:, e, h, :], pw[:, e % 2, h, :],
                                     start=(e == 0 and h == 0), stop=(e == NE - 1 and h == HB - 1))
                if e == 0:
                    for part in (b2_hi, b2_lo):
                        last = pe.matmul(bank[:, Y2, :], part[:], wT[:, bass.ds(u * UT, UT)],
                                         start=False, stop=False)
                last.then_inc(y2_done, 1)

            def turn_y(v):
                pe.wait_ge(yT_done, v + 1)
                if not isinstance(v, int) or v >= 1:
                    pe.wait_ge(o_done, v)
                turn_four(bank[:, TR, :], lambda i: yT[:, i * P:(i + 1) * P], tr_done)

            def group(u, first):
                for e in range(NE):
                    s = u * NE + e
                    if not (first and e < 2):
                        pe.wait_ge(wb_done, s - 1)
                    mlp1_half(u, s, e, 0, first)
                    weights_out(u, e)
                    mlp1_half(u, s, e, 1, first)
                    if e >= 2:
                        mlp2(u, s - 2, e - 2, first)
                    elif not first:
                        mlp2(u - 1, s - 2, e + NE - 2, False)
                    if e == 2 and not first:
                        turn_y(u - 1)

            pe.wait_ge(setup, 3)
            pe.wait_ge(w1_split, NE)
            pe.wait_ge(tT_split, NU)
            pe.wait_ge(wT_done, NU)
            pe.wait_ge(w2_in, 16)
            group(0, True)
            with pe.Fori(1, NU) as u:
                group(u, False)
            mlp2(NU - 1, NU * NE - 2, NE - 2, False)
            mlp2(NU - 1, NU * NE - 1, NE - 1, False)
            turn_y(NU - 1)


def kernel(**inputs):
    import concourse.bacc as bacc
    from concourse.bass_utils import run_bass_kernel_spmd

    a = {k.split("_", 2)[2]: np.asarray(v) for k, v in inputs.items()}
    f = a["x"].dtype
    wab = np.zeros((P, 2, BG, P), f)
    wc4 = np.zeros((P, BG * D), f)
    for i in range(BG):
        wab[:, 0, i, i * NS:(i + 1) * NS] = a["Wa_w"].T
        wab[:, 1, i, i * NS:(i + 1) * NS] = a["WB_w"].T
        wc4[i * NS:(i + 1) * NS, i * D:(i + 1) * D] = a["WC_w"].T
    arrays = {
        "x": a["x"],
        "wab": wab,
        "bab": np.stack([np.tile(a["Wa_b"], BG), np.tile(a["WB_b"], BG)], 1),
        "log_gamma": a["log_gamma"].reshape(1, 1),
        "wc4": wc4,
        "rows2": np.stack([a["D_skip"], a["WC_b"]]),
        "cols3": np.stack([a["ln_w"], a["ln_b"], a["norm_scale"]], 1),
        "gate_w": a["gate_w"],
        "gate_b": a["gate_b"].reshape(1, NE),
        "w1": a["mlp1_w"].reshape(NE, D, HB * P, 2).transpose(1, 0, 3, 2).reshape(P, NE, 2 * HB * P),
        "b1": a["mlp1_b"].reshape(NE, HB, P, 2).transpose(2, 0, 3, 1),
        "w2": a["mlp2_w"].reshape(NE, HB, P, D).transpose(2, 0, 1, 3),
        "b2x2": np.concatenate([a["mlp2_b"], a["mlp2_b"]]),
    }
    arrays |= {k: v.astype(np.float32) for k, v in shape_constants().items()}
    order = ["x", "wab", "bab", "log_gamma", "wc4", "rows2", "cols3", "gate_w", "gate_b", "w1", "b1",
             "w2", "b2x2", "ident", "dft", "idft", "select", "rank"]
    nc = bacc.Bacc("TRN2", target_bir_lowering=False, num_devices=1)
    feeds, args = {}, []
    for name in order:
        arr = np.ascontiguousarray(arrays[name])
        feeds[f"in_{name}"] = arr
        args.append(nc.dram_tensor(f"in_{name}", arr.shape, mybir.dt.from_np(arr.dtype),
                                   kind="ExternalInput").ap())
    args.append(nc.dram_tensor("out_0", (B, T, D), F32, kind="ExternalOutput").ap())
    build(nc, *args)
    r = run_bass_kernel_spmd(nc, [feeds], core_ids=[0])
    return r.results[0]["out_0"]
```

```python
from contextlib import ExitStack

import numpy as np
import concourse.bass as bass
from concourse import mybir

ALU = mybir.AluOpType
ACT = mybir.ActivationFunctionType
AX = mybir.AxisListType
F32 = mybir.dt.float32
F32R = mybir.dt.float32r
I32 = mybir.dt.int32

P = 128
B, T, D = 8, 512, 128
NS = 32
BG = 4
NG = B // BG
TT = T // P
NU = NG * TT
UT = BG * P
NE = 8
HB = 2
L = 8
C1 = T // L
C2 = C1 // L
KB = NS // 2 - 1
EPS = 1e-5
ALPHA = 1.702
LIMIT = 7.0
NBANK = 8


def shape_constants():
    dft = np.zeros((P, 2, NG, P))
    idft = np.zeros((P, 2, NG, P))
    n = np.arange(NS)
    for b in range(B):
        g, i = divmod(b, BG)
        rows = slice(i * NS, i * NS + NS)
        for plane, sign in ((0, np.ones(NS)), (1, (-1.0) ** n)):
            dft[rows, plane, g, b] = sign
            idft[b, plane, g, rows] = sign / NS
        for k in range(1, KB + 1):
            r = B + b * KB + k - 1
            cos, sin = np.cos(2 * np.pi * k * n / NS), np.sin(2 * np.pi * k * n / NS)
            dft[rows, 0, g, r], dft[rows, 1, g, r] = cos, -sin
            idft[r, 0, g, rows], idft[r, 1, g, rows] = 2 * cos / NS, -2 * sin / NS
    select = np.zeros((2 * NE, NE, P))
    for e in range(NE):
        select[e, e], select[e + NE, e] = 1.0, 1.0
    rank = np.tile(NE - np.arange(NE), (P, 1))
    return {"ident": np.eye(P), "dft": dft, "idft": idft, "select": select, "rank": rank}


def build(nc, x, wab, bab, log_gamma, wc4, rows2, cols3, gate_w, gate_b, w1, b1, w2, b2x2,
          ident, dft, idft, select, rank, out):
    with ExitStack() as ctx:
        def sb(name, shape, dt=F32):
            return ctx.enter_context(nc.sbuf_tensor(name, shape, dt))

        def sem(name):
            return ctx.enter_context(nc.semaphore(name))

        bank = ctx.enter_context(nc.psum_tensor("bank", [P, NBANK, 512], F32))

        X = sb("X", [P, NU, BG, D])
        R = sb("R", [P, NU, BG, D])
        bab_s = sb("bab_s", [P, 2])
        gam = sb("gam", [P, 2])
        wc4_s = sb("wc4_s", [P, BG * D])
        rows_s = sb("rows_s", [P, 2, D])
        cols_s = sb("cols_s", [P, 3])
        gate_ws = sb("gate_ws", [P, NE])
        gate_bs = sb("gate_bs", [P, NE])
        rank_s = sb("rank_s", [P, NE])
        ident_s = sb("ident_s", [P, P])
        dft_s = sb("dft_s", [P, 2, NG, P])
        dftg = sb("dftg", [P, 2, NG, P])
        idft_s = sb("idft_s", [P, 2, NG, P])
        w1_hi = sb("w1_hi", [P, NE, 2 * HB * P], F32R)
        w1_lo = sb("w1_lo", [P, NE, 2 * HB * P], F32R)
        w2_hi = sb("w2_hi", [P, NE, HB * D], F32R)
        w2_lo = sb("w2_lo", [P, NE, HB * D], F32R)
        b1_s = sb("b1_s", [P, NE, 2, HB])
        b2_hi = sb("b2_hi", [2 * NE, D], F32R)
        b2_lo = sb("b2_lo", [2 * NE, D], F32R)
        sel_r = sb("sel_r", [2 * NE, NE, P], F32R)
        st = sb("st", [P, 2, BG, 6])
        mv = sb("mv", [P, 3, B, BG, 2])
        nrm = sb("nrm", [P, 3, B, 6, BG])
        half = sb("half", [P, 2 * BG])
        a2 = sb("a2", [P, 3, C1])
        S2 = sb("S2", [P, 4, C1])
        a3 = sb("a3", [P, 3, C2])
        S3 = sb("S3", [P, 2, C2])
        tT_hi = sb("tT_hi", [P, NU * UT], F32R)
        tT_lo = sb("tT_lo", [P, NU * UT], F32R)
        pw_hi = sb("pw_hi", [P, 2, HB, UT], F32R)
        pw_lo = sb("pw_lo", [P, 2, HB, UT], F32R)
        NT = NU * BG
        m12 = sb("m12", [P, 6, NT])
        whi = sb("whi", [P, NT, NE], F32R)
        wT = sb("wT", [2 * NE, NU * UT], F32R)

        au = sb("au", [P, 2, NG, T])
        pr = sb("pr", [P, 2, 2, L * C1])
        acuc = sb("acuc", [P, 5, L, C1])
        xnT = sb("xnT", [P, 2, T])
        Z = sb("Z", [P, 2, BG, D])
        tT = sb("tT", [P, 2, UT])
        wab_s = sb("wab_s", [P, 2, BG, P])

        def part(tensor, start, *shape):
            names = "abcd"[:len(tensor.shape) - 1]
            flat = tensor[:].rearrange(f"p {' '.join(names)} -> p ({' '.join(names)})")
            names = "abcd"[:len(shape)]
            return flat[:, start:start + int(np.prod(shape))].rearrange(
                f"p ({' '.join(names)}) -> p {' '.join(names)}", **dict(zip(names, shape)))

        w_st = part(pr, 0, 4, 512)
        sel_s = part(tT, 0, NE, P)[0:2 * NE]
        b2_s = part(S2, 0, D)[0:2 * NE]
        acol, ucol = acuc[:, 0:3, :, :], acuc[:, 3:5, :, :]
        sq, gt = pr[:, 0, :, :], pr[:, 1, 0, :]
        S = part(au, 0, 4, L, C1)
        areal = part(wab_s, 0, 2, T)[0:B]
        ureal = part(Z, 0, 2, T)[0:B]
        hreal = xnT[0:B, :, :]
        hT = part(acuc, 0, NG, T)
        TE = NT * NE
        lg = part(pr, 0, 2, NT, NE)
        oh = part(pr, 2 * TE, 2, NT, NE)
        eq = part(xnT, 0, NT, NE)
        wtok = part(xnT, TE, NT, NE)
        whl = part(xnT, 2 * TE, NT, 2 * NE)
        gact = au
        lin = part(acuc, 0, 2, HB, UT)
        prod = pr
        pw = [part(Z, 0, HB, UT), part(wab_s, 0, HB, UT)]
        wb = [part(dft_s, 0, 1, UT), part(dftg, 0, 1, UT)]
        yT = part(xnT, 0, UT)
        O = part(tT, 0, BG, D)
        fin = part(tT, UT, BG, D)

        x_in = [sem(f"x_in{b}") for b in range(B)]
        first_in = sem("first_in")
        small_in = sem("small_in")
        w_in = [sem(f"w_in{k}") for k in range(4)]
        w_split = sem("w_split")
        setup = sem("setup")
        gam_sig = sem("gam_sig")
        gam_scaled = sem("gam_scaled")
        half_set = sem("half_set")
        dve_chain = sem("dve_chain")
        pool_chain = sem("pool_chain")
        x_stats = sem("x_stats")
        x_scales = sem("x_scales")
        z_done = sem("z_done")
        zT_done = sem("zT_done")
        xn_done = sem("xn_done")
        proj_done = sem("proj_done")
        r0_done = sem("r0_done")
        skip_done = sem("skip_done")
        a_done = sem("a_done")
        u_done = sem("u_done")
        ahat_done = sem("ahat_done")
        uhat_done = sem("uhat_done")
        sq_done = sem("sq_done")
        mag2_done = sem("mag2_done")
        mag_done = sem("mag_done")
        guard_done = sem("guard_done")
        gate_done = sem("gate_done")
        ucol_done = sem("ucol_done")
        scan_done = sem("scan_done")
        ih_done = sem("ih_done")
        hT_done = sem("hT_done")
        y_done = sem("y_done")
        y_read = sem("y_read")
        y_stats = sem("y_stats")
        y_scales = sem("y_scales")
        yn_done = sem("yn_done")
        x1_done = sem("x1_done")
        x1_stats = sem("x1_stats")
        x1_scales = sem("x1_scales")
        t_done = sem("t_done")
        tTr_done = sem("tTr_done")
        tT_done = sem("tT_done")
        tT_split = sem("tT_split")
        r1_done = sem("r1_done")
        logit_done = sem("logit_done")
        gap_done = sem("gap_done")
        prob_done = sem("prob_done")
        whl_done = sem("whl_done")
        wTr_done = sem("wTr_done")
        wT_done = sem("wT_done")
        gl_ready = sem("gl_ready")
        w_ready = sem("w_ready")
        g_done = sem("g_done")
        l_done = sem("l_done")
        silu_done = sem("silu_done")
        wb_done = sem("wb_done")
        p_done = sem("p_done")
        hi_done = sem("hi_done")
        lo0_done = sem("lo0_done")
        lo1_done = sem("lo1_done")
        pw_done = sem("pw_done")
        y2_done = sem("y2_done")
        yT_done = sem("yT_done")
        tr_done = sem("tr_done")
        clip_done = sem("clip_done")
        o_done = sem("o_done")
        o_bn = sem("o_bn")
        o_stats = sem("o_stats")
        o_pow = sem("o_pow")
        o_neg = sem("o_neg")
        o_scale = sem("o_scale")
        on_done = sem("on_done")
        fin_done = sem("fin_done")
        fin_free = sem("fin_free")
        out_done = sem("out_done")

        block = ctx.enter_context(nc.Block())
        NFIRST, NSMALL = 4, 11

        def zT_bank(n):
            return bank[:, n % 2, :]

        A_BANK, U_BANK, AHAT, UHAT, HT_BANK = 2, 3, 6, 2, 0
        Y_BANKS, LOGITS = 4, 2
        Y2, WB, TR = 4, 5, 7

        def tile_of(b, j):
            return (b // BG) * TT + j, b % BG

        out_v = out.rearrange("(g i) (j p) d -> p g j i d", g=NG, p=P)

        @block.sync
        def _(sp):
            for b in range(B):
                g, i = divmod(b, BG)
                sp.dma_start(X[:, g * TT:(g + 1) * TT, i, :],
                             x[b].rearrange("(j p) d -> p j d", p=P)).then_inc(x_in[b], 16)
            for n in range(2 * NE):
                if n >= 4:
                    sp.wait_ge(w_split, n - 3)
                src = w1[:, n, :] if n < NE else w2[:, n - NE, :]
                sp.dma_start(w_st[:, n % 4, 0:src.shape[1]], src).then_inc(w_in[n % 4], 16)

            sp.sem_inc(fin_free)
            for u in range(NU):
                sp.wait_ge(fin_done, u + 1)
                sp.dma_start(out_v[:, u // TT, u % TT, :, :], fin[:]).then_inc(out_done, 16)
                sp.wait_ge(out_done, 16 * (u + 1))
                if u < NU - 1:
                    sp.sem_inc(fin_free)

        @block.gpsimd
        def _(pool):
            chain = [0]

            def link(ins):
                chain[0] += 1
                ins.then_inc(pool_chain, 1)
                pool.wait_ge(pool_chain, chain[0])

            pool.memset(half[:], -0.5).then_inc(half_set, 1)
            pool.wait_ge(half_set, 1)

            def one_scale(which, n, done):
                v = nrm[:, which, n, :, :]
                link(pool.tensor_tensor(v[:, 2, :], v[:, 0, :], half[:, 0:BG], ALU.pow))
                pool.tensor_tensor(v[:, 5, :], v[:, 4, :], v[:, 2, :], ALU.mult).then_inc(done, 1)

            def two_scales(which, n, done):
                v = nrm[:, which, n, :, :]
                link(pool.tensor_tensor(v[:, 2:4, :], v[:, 0:2, :],
                                        half[:].rearrange("p (a b) -> p a b", a=2), ALU.pow))
                pool.tensor_tensor(v[:, 5, :], v[:, 4, :], v[:, 2, :], ALU.mult).then_inc(done, 1)

            def skip_term(b):
                g, i = divmod(b, BG)
                r = R[:, g * TT:(g + 1) * TT, i, :]
                pool.wait_ge(r0_done, TT * (b + 1))
                link(pool.tensor_tensor(r, r, rows_s[:, 0:1, :].to_broadcast([P, TT, D]), ALU.mult))
                pool.tensor_tensor(r, r, rows_s[:, 1:2, :].to_broadcast([P, TT, D]),
                                   ALU.add).then_inc(skip_done, 1)

            for b in range(B):
                pool.wait_ge(x_stats, b + 1)
                two_scales(0, b, x_scales)
            pool.wait_ge(small_in, 16 * NSMALL)
            for b in range(B):
                skip_term(b)

            for n in range(NU + 2):
                if n < NU:
                    pool.wait_ge(y_stats, n + 1)
                    one_scale(1, n, y_scales)
                if 1 <= n <= NU:
                    pool.wait_ge(yn_done, BG * n)
                    pool.tensor_tensor(X[:, n - 1, :, :], X[:, n - 1, :, :], R[:, n - 1, :, :],
                                       ALU.add).then_inc(x1_done, 1)
                if n >= 2:
                    pool.wait_ge(x1_stats, n - 1)
                    two_scales(2, n - 2, x1_scales)

            def weigh(s, e, reused):
                pool.wait_ge(p_done, s + 1)
                pool.wait_ge(wb_done, s + 1)
                if reused:
                    pool.wait_ge(lo0_done, s - 1)
                    pool.wait_ge(lo1_done, s - 1)
                for h in range(HB):
                    pool.tensor_tensor(pw[e % 2][:, h, :], prod[:, e % 2, h, :], wb[e % 2][:, 0, :],
                                       ALU.mult).then_inc(pw_done, 1)

            def low_half(s, e):
                pool.wait_ge(hi_done, s * 2 + 1)
                pool.tensor_tensor(pw_lo[:, e % 2, 0, :], pw[e % 2][:, 0, :],
                                   pw_hi[:, e % 2, 0, :].bitcast(F32), ALU.subtract).then_inc(lo0_done, 1)

            def out_scale(v):
                pool.wait_ge(o_stats, v + 1)
                w = nrm[:, 0, 0, :, :]
                pool.tensor_tensor(w[:, 2, :], w[:, 0, :], half[:, 0:BG], ALU.pow).then_inc(o_pow, 1)
                pool.wait_ge(o_pow, v + 1)
                pool.tensor_tensor(w[:, 5, :], w[:, 4, :], w[:, 2, :], ALU.mult).then_inc(o_scale, 1)

            def group(u, first):
                for e in range(NE):
                    s = u * NE + e
                    weigh(s, e, not (first and e < 2))
                    low_half(s, e)
                    if not first and e == 4:
                        out_scale(u - 1)

            group(0, True)
            with pool.Fori(1, NU) as u:
                group(u, False)
            out_scale(NU - 1)

        @block.scalar
        def _(act):
            first = [(ident_s[:], ident), (cols_s[:], cols3), (wab_s[:], wab), (bab_s[:], bab)]
            rest = [(gam[:, 0:1], log_gamma.to_broadcast([P, 1])), (dft_s[:], dft),
                    (rows_s[:], rows2.rearrange("(o r) d -> o r d", o=1).to_broadcast([P, 2, D])),
                    (sel_s, select), (b1_s[:], b1), (b2_s[:], b2x2),
                    (idft_s[:], idft), (wc4_s[:], wc4), (gate_ws[:], gate_w),
                    (gate_bs[:], gate_b.to_broadcast([P, NE])), (rank_s[:], rank)]
            assert len(first) == NFIRST and len(rest) == NSMALL
            for loads, arrived in ((first, first_in), (rest, small_in)):
                for dst, src in loads:
                    act.dma_start(dst, src).then_inc(arrived, 16)

            def normal_x(b):
                for j in range(TT):
                    u, i = tile_of(b, j)
                    if j == 0:
                        act.wait_ge(x_scales, b + 1)
                    act.activation(R[:, u, i, :], X[:, u, i, :], ACT.Identity,
                                   bias=nrm[:, 0, b, 5, j:j + 1],
                                   scale=nrm[:, 0, b, 2, j:j + 1]).then_inc(r0_done, 1)

            def turn_x(b):
                act.wait_ge(zT_done, b + 1)
                if b >= 2:
                    act.wait_ge(proj_done, b - 1)
                act.activation(xnT[:, b % 2, :], zT_bank(b), ACT.Identity, bias=cols_s[:, 1:2],
                               scale=cols_s[:, 0:1]).then_inc(xn_done, 1)

            act.wait_ge(first_in, 16 * NFIRST)
            for b in range(B + 1):
                if b >= 1:
                    turn_x(b - 1)
                if b in (BG + 1, B):
                    g = 0 if b == BG + 1 else 1
                    act.wait_ge(proj_done, BG * (g + 1))
                    act.activation(au[:, 0, g, :], bank[:, A_BANK + 2 * g, :], ACT.Tanh,
                                   bias=bab_s[:, 0:1]).then_inc(a_done, 1)
                    act.activation(au[:, 1, g, :], bank[:, U_BANK + 2 * g, :], ACT.Identity,
                                   bias=bab_s[:, 1:2]).then_inc(u_done, 1)
                if b == BG:
                    act.wait_ge(small_in, 16 * NSMALL)
                    act.activation(gam[:, 1:2], gam[:, 0:1], ACT.Sigmoid).then_inc(gam_sig, 1)
                if b < B:
                    normal_x(b)

            act.wait_ge(ahat_done, 1)
            act.wait_ge(w_split, 2 * NE)
            act.activation(sq[:], bank[:, AHAT:AHAT + 2, :], ACT.Square).then_inc(sq_done, 1)
            act.activation(areal[:], bank[0:B, AHAT:AHAT + 2, :], ACT.Abs).then_inc(sq_done, 1)
            act.wait_ge(mag2_done, 1)
            act.activation(gt[:], gt[:], ACT.Sqrt).then_inc(mag_done, 1)
            act.wait_ge(guard_done, 2)
            act.activation(gt[:], gt[:], ACT.Sigmoid, bias=2.0, scale=-2.0).then_inc(gate_done, 1)
            act.activation(areal[:], areal[:], ACT.Sigmoid, bias=2.0, scale=-2.0).then_inc(gate_done, 1)
            act.wait_ge(uhat_done, 1)
            act.activation(ureal[:], bank[0:B, UHAT:UHAT + 2, :], ACT.Identity).then_inc(ucol_done, 1)
            act.activation(ucol[:], bank[:, UHAT:UHAT + 2, :].rearrange("p r (c l) -> p r l c", l=L),
                           ACT.Identity).then_inc(ucol_done, 1)

            for g in range(NG):
                act.wait_ge(ih_done, g + 1)
                act.activation(hT[:, g, :].rearrange("p (c l) -> p l c", l=L),
                               bank[:, HT_BANK + g, :].rearrange("p (l c) -> p l c", l=L),
                               ACT.Identity).then_inc(hT_done, 1)

            for n in range(NU + 4):
                if n < NU:
                    act.wait_ge(y_scales, n + 1)
                    for i in range(BG):
                        act.activation(R[:, n, i, :], R[:, n, i, :], ACT.Identity,
                                       bias=nrm[:, 1, n, 5, i:i + 1],
                                       scale=nrm[:, 1, n, 2, i:i + 1]).then_inc(yn_done, 1)
                if 2 <= n < NU + 2:
                    m = n - 2
                    act.wait_ge(x1_scales, m + 1)
                    for i in range(BG):
                        act.activation(R[:, m, i, :], X[:, m, i, :], ACT.Identity,
                                       bias=nrm[:, 2, m, 5, i:i + 1],
                                       scale=nrm[:, 2, m, 2, i:i + 1]).then_inc(r1_done, 1)
                if 3 <= n < NU + 3:
                    m = n - 3
                    act.wait_ge(tTr_done, m + 1)
                    if m >= 2:
                        act.wait_ge(tT_split, m - 1)
                        act.wait_ge(logit_done, m - 1)
                    act.activation(tT[:, m % 2, :], zT_bank(m), ACT.Identity,
                                   scale=cols_s[:, 2:3]).then_inc(tT_done, 1)
                    act.activation(tT_hi[:, m * UT:(m + 1) * UT], zT_bank(m), ACT.Identity,
                                   scale=cols_s[:, 2:3]).then_inc(tT_done, 1)

            act.wait_ge(gap_done, 2)
            act.activation(m12[:, 4:6, :], m12[:, 2:4, :], ACT.Sigmoid).then_inc(prob_done, 1)

            def weights_in(n):
                act.wait_ge(wTr_done, n + 1)
                act.activation(wT[:, n * UT:(n + 1) * UT], bank[0:2 * NE, TR, :],
                               ACT.Identity).then_inc(wT_done, 1)

            weights_in(0)

            def linear_half(s, e, h, first):
                k = s * 2 + h
                act.wait_ge(gl_ready, k + 1)
                if h == 0 and not (first and e < 2):
                    act.wait_ge(p_done, s - 1)
                act.activation(lin[:, e % 2, h, :], bank[:, 2 * h + 1, :], ACT.Identity,
                               bias=b1_s[:, e, 1, h:h + 1]).then_inc(l_done, 1)

            def high_half(s, e, h, reused):
                act.wait_ge(pw_done, s * 2 + h + 1)
                if reused and h == 0:
                    act.wait_ge(y2_done, s - 1)
                act.activation(pw_hi[:, e % 2, h, :], pw[e % 2][:, h, :], ACT.Identity).then_inc(hi_done, 1)

            def evacuate_y(v):
                act.wait_ge(y2_done, (v + 1) * NE)
                act.activation(yT[:], bank[:, Y2, :], ACT.Identity).then_inc(yT_done, 1)

            def out_norm(v):
                act.wait_ge(o_scale, v + 1)
                for i in range(BG):
                    act.activation(O[:, i, :], O[:, i, :], ACT.Identity, bias=nrm[:, 0, 0, 5, i:i + 1],
                                   scale=nrm[:, 0, 0, 2, i:i + 1]).then_inc(on_done, 1)

            def group(u, first):
                for e in range(NE):
                    s = u * NE + e
                    act.wait_ge(w_ready, s + 1)
                    if not (first and e < 2):
                        act.wait_ge(pw_done, s * 2 - 2)
                    act.activation(wb[e % 2][:, 0, :], bank[:, WB + e % 2, :], ACT.Copy,
                                   scale=1.0 / ALPHA).then_inc(wb_done, 1)
                    if e == 3 and not first:
                        evacuate_y(u - 1)
                    linear_half(s, e, 0, first)
                    if not (first and e < 2):
                        high_half(s - 2, (e - 2) % NE, 1, not (first and e < 4))
                    linear_half(s, e, 1, first)
                    act.wait_ge(g_done, s * 2 + 2)
                    act.activation(gact[:, e % 2, :, :], gact[:, e % 2, :, :], ACT.Silu,
                                   scale=ALPHA).then_inc(silu_done, 1)
                    if not (first and e == 0):
                        high_half(s - 1, (e - 1) % NE, 0, not (first and e < 3))
                    if first and e < NU - 1:
                        weights_in(e + 1)
                    if e == 6 and not first:
                        out_norm(u - 1)

            group(0, True)
            with act.Fori(1, NU) as u:
                group(u, False)
            high_half(NU * NE - 2, NE - 2, 1, True)
            high_half(NU * NE - 1, NE - 1, 0, True)
            high_half(NU * NE - 1, NE - 1, 1, True)
            evacuate_y(NU - 1)
            out_norm(NU - 1)

        @block.vector
        def _(dve):
            chain = [0]

            def link(ins):
                chain[0] += 1
                ins.then_inc(dve_chain, 1)
                dve.wait_ge(dve_chain, chain[0])

            def loose(ins):
                chain[0] += 1
                ins.then_inc(dve_chain, 1)
                return chain[0]

            def stats(tiles, which, n, done):
                last = [loose(dve.bn_stats(st[:, n % 2, k, :], tl)) for k, tl in enumerate(tiles)]
                for k in range(BG):
                    dve.wait_ge(dve_chain, last[k])
                    end = loose(dve.bn_aggr(mv[:, which, n, k, :], st[:, n % 2, k, :]))
                dve.wait_ge(dve_chain, end)
                v, m = nrm[:, which, n, :, :], mv[:, which, n, :, :]
                loose(dve.tensor_scalar(v[:, 0, :], m[:, :, 1], EPS, None, ALU.add))
                if which != 1:
                    loose(dve.tensor_scalar(v[:, 1, :], m[:, :, 1], 1.0 + EPS, EPS * EPS,
                                            ALU.mult, ALU.add))
                dve.tensor_scalar(v[:, 4, :], m[:, :, 0], -1.0, None, ALU.mult).then_inc(done, 1)

            def scaled(dst, src, which, n, k, col, done):
                dve.tensor_scalar(dst, src, mv[:, which, n, k, 0:1], nrm[:, which, n, col, k:k + 1],
                                  ALU.subtract, ALU.mult).then_inc(done, 1)

            def split_weights(n):
                dve.wait_ge(w_in[n % 4], 16 * (n // 4 + 1))
                hi, lo = (w1_hi[:, n, :], w1_lo[:, n, :]) if n < NE else (w2_hi[:, n - NE, :], w2_lo[:, n - NE, :])
                wv = w_st[:, n % 4, 0:hi.shape[1]]
                link(dve.tensor_copy(hi, wv))
                dve.tensor_tensor(lo, wv, hi.bitcast(F32), ALU.subtract).then_inc(w_split, 1)

            for b in range(B + 1):
                if b >= BG:
                    split_weights(b - BG)
                if b < B:
                    dve.wait_ge(x_in[b], 16)
                    stats([X[:, tile_of(b, j)[0], b % BG, :] for j in range(TT)], 0, b, x_stats)
                if b >= 1:
                    a = b - 1
                    dve.wait_ge(x_scales, a + 1)
                    if a >= 2:
                        dve.wait_ge(zT_done, a - 1)
                    for j in range(TT):
                        scaled(Z[:, a % 2, j, :], X[:, tile_of(a, j)[0], a % BG, :], 0, a, j, 3, z_done)
                if b == BG + 1:
                    dve.wait_ge(gam_sig, 1)
                    dve.tensor_scalar(dftg[:], dft_s[:], gam[:, 1:2], None, ALU.mult).then_inc(gam_scaled, 1)
            for n in range(B - BG + 1, 2 * NE):
                split_weights(n)
            dve.tensor_scalar(b1_s[:, :, 1, :], b1_s[:, :, 1, :], 1.0, None, ALU.add).then_inc(setup, 1)
            dve.tensor_copy(sel_r[:], sel_s[:]).then_inc(setup, 1)
            link(dve.tensor_copy(b2_hi[:], b2_s[:]))
            dve.tensor_tensor(b2_lo[:], b2_s[:], b2_hi[:].bitcast(F32), ALU.subtract).then_inc(setup, 1)

            dve.wait_ge(sq_done, 2)
            dve.tensor_tensor(gt[:], sq[:, 0, :], sq[:, 1, :], ALU.add).then_inc(mag2_done, 1)
            dve.tensor_scalar(areal[:], areal[:], 1e-8, None, ALU.max).then_inc(guard_done, 1)
            dve.wait_ge(mag_done, 1)
            dve.tensor_scalar(gt[:], gt[:], 1e-8, None, ALU.max).then_inc(guard_done, 1)
            dve.wait_ge(gate_done, 2)

            def chunked(ap):
                return ap.rearrange("p (c l) -> p l c", l=L)

            are, aim = bank[:, AHAT, :], bank[:, AHAT + 1, :]
            loose(dve.tensor_tensor(acol[:, 0, :, :], chunked(are), chunked(gt[:]), ALU.mult))
            loose(dve.tensor_tensor(acol[:, 2, :, :], chunked(aim), chunked(gt[:]), ALU.mult))
            link(dve.tensor_tensor(areal[:], bank[0:B, AHAT:AHAT + 2, :], areal[:], ALU.mult))
            dve.tensor_scalar(acol[:, 1, :, :], acol[:, 2, :, :], -1.0, None, ALU.mult)\
               .then_inc(dve_chain, 1)
            chain[0] += 1
            dve.wait_ge(ucol_done, 2)
            for r in range(2):
                end = loose(dve.tensor_tensor_scan(hreal[:, r, :], areal[:, r, :], ureal[:, r, :], 0.0,
                                                   ALU.mult, ALU.add))

            def scan_level(a, u, s, steps, width, planes):
                ks = planes // 2
                loose(dve.tensor_copy(s(0)[:, 0:2, :], u(0)))
                if ks == 2:
                    loose(dve.tensor_copy(s(0)[:, 2:3, :], a(0)[:, 0:1, :]))
                    loose(dve.tensor_copy(s(0)[:, 3:4, :], a(0)[:, 2:3, :]))
                for l in range(1, steps):
                    p1 = pr[:, 0, :, :].rearrange("p a b -> p (a b)")[:, 0:planes * width]
                    p2 = pr[:, 1, :, :].rearrange("p a b -> p (a b)")[:, 0:planes * width]
                    v1 = p1.rearrange("p (k w) -> p k w", k=planes)
                    v2 = p2.rearrange("p (k w) -> p k w", k=planes)
                    dve.wait_ge(dve_chain, chain[0])
                    loose(dve.tensor_tensor(v1, a(l)[:, 0:1, :].to_broadcast([P, planes, width]),
                                            s(l - 1), ALU.mult))
                    for j in range(2):
                        end = loose(dve.tensor_tensor(
                            v2[:, j:planes:2, :], a(l)[:, 1 + j:2 + j, :].to_broadcast([P, ks, width]),
                            s(l - 1)[:, 1 - j:planes:2, :], ALU.mult))
                    dve.wait_ge(dve_chain, end - 2)
                    loose(dve.tensor_tensor(v1[:, 0:2, :], v1[:, 0:2, :], u(l), ALU.add))
                    dve.wait_ge(dve_chain, chain[0])
                    loose(dve.tensor_tensor(s(l), v1, v2, ALU.add))
                dve.wait_ge(dve_chain, chain[0])

            def carry_level(s, carry, groups, width):
                n = groups * width
                p1 = pr[:, 0, :, 0:n].rearrange("p r (l c) -> p r l c", l=groups)
                p2 = pr[:, 1, :, 0:n].rearrange("p r (l c) -> p r l c", l=groups)
                for r in range(2):
                    bc = carry[:, r:r + 1, :].to_broadcast([P, groups, width])
                    loose(dve.tensor_tensor(p1[:, r, :, :], s[:, 2, :, :], bc, ALU.mult))
                    loose(dve.tensor_tensor(p2[:, r, :, :], s[:, 3, :, :], bc, ALU.mult))
                dve.wait_ge(dve_chain, chain[0] - 2)
                loose(dve.tensor_tensor(p1[:, 0, :, :], p1[:, 0, :, :], s[:, 0, :, :], ALU.add))
                dve.wait_ge(dve_chain, chain[0] - 1)
                loose(dve.tensor_tensor(p1[:, 1, :, :], p1[:, 1, :, :], s[:, 1, :, :], ALU.add))
                dve.wait_ge(dve_chain, chain[0] - 1)
                loose(dve.tensor_tensor(s[:, 0, :, :], p1[:, 0, :, :], p2[:, 1, :, :], ALU.subtract))
                dve.wait_ge(dve_chain, chain[0] - 1)
                loose(dve.tensor_tensor(s[:, 1, :, :], p1[:, 1, :, :], p2[:, 0, :, :], ALU.add))
                dve.wait_ge(dve_chain, chain[0])

            def ends(s, a):
                loose(dve.tensor_copy(a[:, 0:1, :], s[:, 2:3, :]))
                loose(dve.tensor_scalar(a[:, 1:2, :], s[:, 3:4, :], -1.0, None, ALU.mult))
                loose(dve.tensor_copy(a[:, 2:3, :], s[:, 3:4, :]))
                dve.wait_ge(dve_chain, chain[0])

            scan_level(lambda l: acol[:, :, l, :], lambda l: ucol[:, :, l, :], lambda l: S[:, :, l, :],
                       L, C1, 4)
            ends(S[:, :, L - 1, :], a2)
            end2 = S[:, :, L - 1, :]
            scan_level(lambda l: a2[:, :, l::L], lambda l: end2[:, 0:2, l::L], lambda l: S2[:, :, l::L],
                       L, C2, 4)
            ends(S2[:, :, L - 1::L], a3)
            end3 = S2[:, :, L - 1::L]
            scan_level(lambda l: a3[:, :, l:l + 1], lambda l: end3[:, 0:2, l:l + 1],
                       lambda l: S3[:, :, l:l + 1], C2, 1, 2)
            v2 = S2[:].rearrange("p r (c l) -> p r l c", l=L)
            carry_level(v2[:, :, :, 1:], S3[:, :, 0:C2 - 1], L, C2 - 1)
            carry_level(S[:, :, :, 1:], S2[:, 0:2, 0:C1 - 1], L, C1 - 1)
            dve.tensor_copy(S[0:B, 0:2, :, :], hreal[:].rearrange("p r (c l) -> p r l c", l=L))\
               .then_inc(scan_done, 1)

            def y_in(n):
                dve.wait_ge(y_done, n + 1)
                dve.wait_ge(skip_done, BG * (n // TT + 1))
                dve.tensor_tensor(R[:, n, :, :], bank[:, Y_BANKS + n % 4, :].rearrange("p (i d) -> p i d", d=D),
                                  R[:, n, :, :], ALU.add).then_inc(y_read, 1)
                dve.wait_ge(y_read, n + 1)
                stats([R[:, n, i, :] for i in range(BG)], 1, n, y_stats)

            def x1_stat(n):
                dve.wait_ge(x1_done, n + 1)
                stats([X[:, n, i, :] for i in range(BG)], 2, n, x1_stats)

            def t_norm(n):
                dve.wait_ge(x1_scales, n + 1)
                dve.wait_ge(zT_done, B)
                if n >= 2:
                    dve.wait_ge(tTr_done, n - 1)
                for i in range(BG):
                    scaled(Z[:, n % 2, i, :], X[:, n, i, :], 2, n, i, 3, t_done)

            def t_split(n):
                dve.wait_ge(tT_done, 2 * (n + 1))
                hi, lo = tT_hi[:, n * UT:(n + 1) * UT], tT_lo[:, n * UT:(n + 1) * UT]
                dve.tensor_tensor(lo, tT[:, n % 2, :], hi.bitcast(F32), ALU.subtract).then_inc(tT_split, 1)

            for n in range(NU + 5):
                for lag, stage in ((0, y_in), (2, x1_stat), (3, t_norm), (4, t_split)):
                    if 0 <= n - lag < NU:
                        stage(n - lag)

            dve.wait_ge(logit_done, NU)

            def bc8(v):
                return v.rearrange("p (t o) -> p t o", o=1).to_broadcast([P, NT, NE])

            def bct(v):
                return v.rearrange("p (o e) -> p o e", o=1).to_broadcast([P, NT, NE])

            link(dve.tensor_tensor(lg[:, 0, :, :],
                                   bank[:, LOGITS, 0:NT * NE].rearrange("p (t e) -> p t e", e=NE),
                                   bct(gate_bs[:]), ALU.add))
            for k in range(2):
                link(dve.tensor_reduce(m12[:, k, :], lg[:, k, :, :], AX.X, ALU.max))
                link(dve.tensor_tensor(eq[:], lg[:, k, :, :], bc8(m12[:, k, :]), ALU.is_equal))
                link(dve.tensor_tensor(eq[:], eq[:], bct(rank_s[:]), ALU.mult))
                link(dve.tensor_reduce(m12[:, 4, :], eq[:], AX.X, ALU.max))
                link(dve.tensor_tensor(oh[:, k, :, :], bct(rank_s[:]), bc8(m12[:, 4, :]), ALU.is_equal))
                if k == 0:
                    flat = "p t e -> p (t e)"
                    link(dve.scalar_tensor_tensor(lg[:, 1, :, :].rearrange(flat),
                                                  oh[:, 0, :, :].rearrange(flat), -3.0e38,
                                                  lg[:, 0, :, :].rearrange(flat), ALU.mult, ALU.add))
            dve.tensor_tensor(m12[:, 2, :], m12[:, 0, :], m12[:, 1, :], ALU.subtract).then_inc(gap_done, 1)
            dve.tensor_tensor(m12[:, 3, :], m12[:, 1, :], m12[:, 0, :], ALU.subtract).then_inc(gap_done, 1)
            dve.wait_ge(prob_done, 1)
            link(dve.tensor_tensor(wtok[:], oh[:, 0, :, :], bc8(m12[:, 4, :]), ALU.mult))
            link(dve.tensor_tensor(eq[:], oh[:, 1, :, :], bc8(m12[:, 5, :]), ALU.mult))
            link(dve.tensor_tensor(wtok[:], wtok[:], eq[:], ALU.add))
            link(dve.tensor_copy(whi[:], wtok[:]))
            dve.tensor_copy(whl[:, :, 0:NE], whi[:].bitcast(F32)).then_inc(whl_done, 1)
            dve.tensor_tensor(whl[:, :, NE:2 * NE], wtok[:], whi[:].bitcast(F32),
                              ALU.subtract).then_inc(whl_done, 1)

            def glu_half(s, e, h, reused):
                if reused and h == 0:
                    dve.wait_ge(p_done, s - 1)
                dve.wait_ge(gl_ready, s * 2 + h + 1)
                dve.tensor_scalar(gact[:, e % 2, h, :], bank[:, 2 * h, :], b1_s[:, e, 0, h:h + 1],
                                  LIMIT, ALU.add, ALU.min).then_inc(g_done, 1)

            def clip(s, e):
                dve.wait_ge(l_done, s * 2 + 2)
                dve.tensor_scalar(lin[:, e % 2, :, :], lin[:, e % 2, :, :], LIMIT + 1.0, 1.0 - LIMIT,
                                  ALU.min, ALU.max).then_inc(clip_done, 1)

            def combine(s, e, reused):
                dve.wait_ge(clip_done, s + 1)
                dve.wait_ge(silu_done, s + 1)
                if reused:
                    dve.wait_ge(pw_done, s * 2 - 2)
                dve.tensor_tensor(prod[:, e % 2, :, :], lin[:, e % 2, :, :], gact[:, e % 2, :, :],
                                  ALU.mult).then_inc(p_done, 1)

            def low_half(s, e):
                dve.wait_ge(hi_done, s * 2 + 2)
                dve.tensor_tensor(pw_lo[:, e % 2, 1, :], pw[e % 2][:, 1, :],
                                  pw_hi[:, e % 2, 1, :].bitcast(F32), ALU.subtract).then_inc(lo1_done, 1)

            def out_in(v):
                dve.wait_ge(tr_done, v + 1)
                dve.tensor_tensor(O[:], bank[:, TR, :].rearrange("p (i d) -> p i d", d=D),
                                  R[:, bass.ds(v, 1), :, :].rearrange("p a i d -> p (a i) d"),
                                  ALU.add).then_inc(o_done, 1)
                dve.wait_ge(o_done, v + 1)
                for i in range(BG):
                    dve.bn_stats(st[:, 0, i, :], O[:, i, :]).then_inc(o_bn, 1)

            def out_aggregate(v):
                for i in range(BG):
                    dve.bn_aggr(mv[:, 0, 0, i, :], st[:, 0, i, :]).then_inc(o_bn, 1)
                dve.wait_ge(o_bn, (v + 1) * 2 * BG)
                dve.tensor_scalar(nrm[:, 0, 0, 4, :], mv[:, 0, 0, :, 0], -1.0, None,
                                  ALU.mult).then_inc(o_neg, 1)
                dve.tensor_scalar(nrm[:, 0, 0, 0, :], mv[:, 0, 0, :, 1], EPS, None,
                                  ALU.add).then_inc(o_stats, 1)

            def out_add(v):
                dve.wait_ge(on_done, BG * (v + 1))
                dve.wait_ge(fin_free, v + 1)
                dve.tensor_tensor(fin[:], O[:], X[:, bass.ds(v, 1), :, :].rearrange("p a i d -> p (a i) d"),
                                  ALU.add).then_inc(fin_done, 1)

            def group(u, first):
                for e in range(NE):
                    s = u * NE + e
                    if not first and e == 5:
                        dve.wait_ge(o_bn, (u - 1) * 2 * BG + BG)
                    if not (first and e == 0):
                        clip(s - 1, (e - 1) % NE)
                    glu_half(s, e, 0, not (first and e < 2))
                    if not (first and e == 0):
                        combine(s - 1, (e - 1) % NE, not (first and e < 3))
                    glu_half(s, e, 1, True)
                    if not (first and e < 2):
                        low_half(s - 2, (e - 2) % NE)
                    if not first and e == 4:
                        out_in(u - 1)
                    if not first and e == 5:
                        out_aggregate(u - 1)
                    if not first and e == 7:
                        out_add(u - 1)

            group(0, True)
            with dve.Fori(1, NU) as u:
                group(u, False)
            clip(NU * NE - 1, NE - 1)
            combine(NU * NE - 1, NE - 1, True)
            low_half(NU * NE - 2, NE - 2)
            low_half(NU * NE - 1, NE - 1)
            out_in(NU - 1)
            dve.wait_ge(o_bn, (NU - 1) * 2 * BG + BG)
            out_aggregate(NU - 1)
            out_add(NU - 1)

        @block.tensor
        def _(pe):
            pe.wait_ge(first_in, 16 * NFIRST)

            def turn_four(dst, src, done):
                for i in range(BG):
                    last = pe.transpose(dst[:, i * P:(i + 1) * P], src(i), ident_s[:])
                last.then_inc(done, 1)

            def transform(g):
                for done, to, table, k in ((a_done, AHAT, dftg, 0), (u_done, UHAT, dft_s, 1)):
                    pe.wait_ge(done, g + 1)
                    for r in range(2):
                        last = pe.matmul(bank[:, to + r, :], table[:, r, g, :], au[:, k, g, :],
                                         start=(g == 0), stop=(g == NG - 1))
                    if g == NG - 1:
                        last.then_inc((ahat_done, uhat_done)[k], 1)

            for b in range(B + 1):
                if b < B:
                    pe.wait_ge(z_done, TT * (b + 1))
                    if b >= 2:
                        pe.wait_ge(xn_done, b - 1)
                    turn_four(zT_bank(b), lambda i: Z[:, b % 2, i, :], zT_done)
                if b >= 1:
                    g, i = divmod(b - 1, BG)
                    pe.wait_ge(xn_done, b)
                    for r in range(2):
                        last = pe.matmul(bank[:, A_BANK + 2 * g + r, :], wab_s[:, r, i, :],
                                         xnT[:, (b - 1) % 2, :], start=(i == 0), stop=(i == BG - 1))
                    last.then_inc(proj_done, 1)
                if b == BG + 2:
                    pe.wait_ge(small_in, 16 * NSMALL)
                    pe.wait_ge(gam_scaled, 1)
                    transform(0)
            transform(1)

            pe.wait_ge(scan_done, 1)
            for g in range(NG):
                for r in range(2):
                    last = pe.matmul(bank[:, HT_BANK + g, :], idft_s[:, r, g, :],
                                     S[:, r, :, :].rearrange("p l c -> p (l c)"),
                                     start=(r == 0), stop=(r == 1))
                last.then_inc(ih_done, 1)

            def project(n):
                g, j = divmod(n, TT)
                pe.wait_ge(hT_done, g + 1)
                if n >= 4:
                    pe.wait_ge(y_read, n - 3)
                pe.matmul(bank[:, Y_BANKS + n % 4, :], hT[:, g, j * P:(j + 1) * P], wc4_s[:],
                          start=True, stop=True).then_inc(y_done, 1)

            def turn_t(n):
                pe.wait_ge(t_done, BG * (n + 1))
                pe.wait_ge(hT_done, NG)
                if n >= 2:
                    pe.wait_ge(tT_done, 2 * (n - 1))
                turn_four(zT_bank(n), lambda i: Z[:, n % 2, i, :], tTr_done)

            def logits(n):
                pe.wait_ge(tT_done, 2 * n + 1)
                pe.wait_ge(hT_done, NG)
                for i in range(BG):
                    t = n * BG + i
                    last = pe.matmul(bank[:, LOGITS, t * NE:(t + 1) * NE], tT[:, n % 2, i * P:(i + 1) * P],
                                     gate_ws[:], start=True, stop=True)
                last.then_inc(logit_done, 1)

            for n in range(4):
                project(n)
            for n in range(NU + 1):
                if n + 4 < NU:
                    project(n + 4)
                if n < NU:
                    turn_t(n)
                if n >= 1:
                    logits(n - 1)

            def turn_weights(n):
                if n >= 1:
                    pe.wait_ge(wT_done, n)
                for i in range(BG):
                    last = pe.transpose(bank[0:2 * NE, TR, i * P:(i + 1) * P],
                                        whl[:, n * BG + i, :], ident_s[:])
                last.then_inc(wTr_done, 1)

            pe.wait_ge(whl_done, 2)
            turn_weights(0)

            def weights_out(u, e):
                pe.matmul(bank[:, WB + e % 2, :], sel_r[:, e, :], wT[:, bass.ds(u * UT, UT)],
                          start=True, stop=True).then_inc(w_ready, 1)

            def mlp1_half(u, s, e, h, first):
                k = s * 2 + h
                if not (first and e == 0):
                    pe.wait_ge(g_done, k - 1)
                    pe.wait_ge(l_done, k - 1)
                hi, lo = tT_hi[:, bass.ds(u * UT, UT)], tT_lo[:, bass.ds(u * UT, UT)]
                for r in range(2):
                    dst = bank[:, 2 * h + r, :]
                    c = (r * HB + h) * P
                    whi_, wlo_ = w1_hi[:, e, c:c + P], w1_lo[:, e, c:c + P]
                    pe.matmul(dst, whi_, hi, start=True, stop=False)
                    pe.matmul(dst, whi_, lo, start=False, stop=False)
                    last = pe.matmul(dst, wlo_, hi, start=False, stop=True)
                last.then_inc(gl_ready, 1)

            def mlp2(u, s, e, first):
                if e == 0 and not first:
                    pe.wait_ge(yT_done, u)
                pe.wait_ge(lo0_done, s + 1)
                pe.wait_ge(lo1_done, s + 1)
                y = bank[:, Y2, :]
                for h in range(HB):
                    whi_, wlo_ = w2_hi[:, e, h * D:(h + 1) * D], w2_lo[:, e, h * D:(h + 1) * D]
                    hi, lo = pw_hi[:, e % 2, h, :], pw_lo[:, e % 2, h, :]
                    pe.matmul(y, whi_, hi, start=(e == 0 and h == 0), stop=False)
                    pe.matmul(y, whi_, lo, start=False, stop=False)
                    last = pe.matmul(y, wlo_, hi, start=False, stop=(e == NE - 1 and h == HB - 1))
                if e == 0:
                    for part in (b2_hi, b2_lo):
                        last = pe.matmul(bank[:, Y2, :], part[:], wT[:, bass.ds(u * UT, UT)],
                                         start=False, stop=False)
                last.then_inc(y2_done, 1)

            def turn_y(v):
                pe.wait_ge(yT_done, v + 1)
                turn_four(bank[:, TR, :], lambda i: yT[:, i * P:(i + 1) * P], tr_done)

            def group(u, first):
                for e in range(NE):
                    s = u * NE + e
                    if not (first and e < 2):
                        pe.wait_ge(wb_done, s - 1)
                    mlp1_half(u, s, e, 0, first)
                    weights_out(u, e)
                    mlp1_half(u, s, e, 1, first)
                    if e >= 3:
                        mlp2(u, s - 3, e - 3, first)
                    elif not first:
                        mlp2(u - 1, s - 3, e + NE - 3, False)
                    if e == 3 and not first:
                        turn_y(u - 1)
                    if first and e < NU - 1:
                        turn_weights(e + 1)

            pe.wait_ge(setup, 3)
            pe.wait_ge(w_split, 2 * NE)
            pe.wait_ge(tT_split, NU)
            pe.wait_ge(wT_done, 1)
            group(0, True)
            with pe.Fori(1, NU) as u:
                group(u, False)
            mlp2(NU - 1, NU * NE - 3, NE - 3, False)
            mlp2(NU - 1, NU * NE - 2, NE - 2, False)
            mlp2(NU - 1, NU * NE - 1, NE - 1, False)
            turn_y(NU - 1)


def kernel(**inputs):
    import concourse.bacc as bacc
    from concourse.bass_utils import run_bass_kernel_spmd

    a = {k.split("_", 2)[2]: np.asarray(v) for k, v in inputs.items()}
    f = a["x"].dtype
    wab = np.zeros((P, 2, BG, P), f)
    wc4 = np.zeros((P, BG * D), f)
    for i in range(BG):
        wab[:, 0, i, i * NS:(i + 1) * NS] = a["Wa_w"].T
        wab[:, 1, i, i * NS:(i + 1) * NS] = a["WB_w"].T
        wc4[i * NS:(i + 1) * NS, i * D:(i + 1) * D] = a["WC_w"].T
    arrays = {
        "x": a["x"],
        "wab": wab,
        "bab": np.stack([np.tile(a["Wa_b"], BG), np.tile(a["WB_b"], BG)], 1),
        "log_gamma": a["log_gamma"].reshape(1, 1),
        "wc4": wc4,
        "rows2": np.stack([a["D_skip"], a["WC_b"]]),
        "cols3": np.stack([a["ln_w"], a["ln_b"], a["norm_scale"]], 1),
        "gate_w": a["gate_w"],
        "gate_b": a["gate_b"].reshape(1, NE),
        "w1": a["mlp1_w"].reshape(NE, D, HB * P, 2).transpose(1, 0, 3, 2).reshape(P, NE, 2 * HB * P),
        "b1": a["mlp1_b"].reshape(NE, HB, P, 2).transpose(2, 0, 3, 1),
        "w2": a["mlp2_w"].reshape(NE, HB, P, D).transpose(2, 0, 1, 3).reshape(P, NE, HB * D),
        "b2x2": np.concatenate([a["mlp2_b"], a["mlp2_b"]]),
    }
    arrays |= {k: v.astype(np.float32) for k, v in shape_constants().items()}
    order = ["x", "wab", "bab", "log_gamma", "wc4", "rows2", "cols3", "gate_w", "gate_b", "w1", "b1",
             "w2", "b2x2", "ident", "dft", "idft", "select", "rank"]
    nc = bacc.Bacc("TRN2", target_bir_lowering=False, num_devices=1)
    feeds, args = {}, []
    for name in order:
        arr = np.ascontiguousarray(arrays[name])
        feeds[f"in_{name}"] = arr
        args.append(nc.dram_tensor(f"in_{name}", arr.shape, mybir.dt.from_np(arr.dtype),
                                   kind="ExternalInput").ap())
    args.append(nc.dram_tensor("out_0", (B, T, D), F32, kind="ExternalOutput").ap())
    build(nc, *args)
    r = run_bass_kernel_spmd(nc, [feeds], core_ids=[0])
    return r.results[0]["out_0"]
```

```python
from contextlib import ExitStack

import numpy as np
import concourse.bass as bass
from concourse import mybir

ALU = mybir.AluOpType
ACT = mybir.ActivationFunctionType
AX = mybir.AxisListType
F32 = mybir.dt.float32
F32R = mybir.dt.float32r

P = 128
B, T, D = 8, 512, 128
NS = 32
BG = 4
NG = B // BG
TT = T // P
NU = NG * TT
UT = BG * P
NE = 8
HB = 2
L = 8
C1 = T // L
C2 = C1 // L
KB = NS // 2 - 1
EPS = 1e-5
ALPHA = 1.702
LIMIT = 7.0
NBANK = 8


def shape_constants():
    dft = np.zeros((P, 2, NG, P))
    idft = np.zeros((P, 2, NG, P))
    n = np.arange(NS)
    for b in range(B):
        g, i = divmod(b, BG)
        rows = slice(i * NS, i * NS + NS)
        for plane, sign in ((0, np.ones(NS)), (1, (-1.0) ** n)):
            dft[rows, plane, g, b] = sign
            idft[b, plane, g, rows] = sign / NS
        for k in range(1, KB + 1):
            r = B + b * KB + k - 1
            cos, sin = np.cos(2 * np.pi * k * n / NS), np.sin(2 * np.pi * k * n / NS)
            dft[rows, 0, g, r], dft[rows, 1, g, r] = cos, -sin
            idft[r, 0, g, rows], idft[r, 1, g, rows] = 2 * cos / NS, -2 * sin / NS
    rank = np.tile(NE - np.arange(NE), (P, 1))
    return {"ident": np.eye(P), "dft": dft, "idft": idft, "rank": rank}


def build(nc, x, wab, bab, log_gamma, wc4, rows2, cols3, gate_w, gate_b, w1, b1, w2, b2,
          ident, dft, idft, rank, out, token_weights):
    with ExitStack() as ctx:
        def sb(name, shape, dt=F32):
            return ctx.enter_context(nc.sbuf_tensor(name, shape, dt))

        def sem(name):
            return ctx.enter_context(nc.semaphore(name))

        bank = ctx.enter_context(nc.psum_tensor("bank", [P, NBANK, 512], F32))

        X = sb("X", [P, NU, BG, D])
        R = sb("R", [P, NU, BG, D])
        bab_s = sb("bab_s", [P, 2])
        gam = sb("gam", [P, 2])
        wc4_s = sb("wc4_s", [P, BG * D])
        rows_s = sb("rows_s", [P, 2, D])
        cols_s = sb("cols_s", [P, 3])
        gate_ws = sb("gate_ws", [P, NE])
        gate_bs = sb("gate_bs", [P, NE])
        rank_s = sb("rank_s", [P, NE])
        ident_s = sb("ident_s", [P, P])
        dft_s = sb("dft_s", [P, 2, NG, P])
        dftg = sb("dftg", [P, 2, NG, P])
        idft_s = sb("idft_s", [P, 2, NG, P])
        w1_hi = sb("w1_hi", [P, NE, 2 * HB * P], F32R)
        w1_lo = sb("w1_lo", [P, NE, 2 * HB * P], F32R)
        w2_hi = sb("w2_hi", [P, NE, HB * D], F32R)
        w2_lo = sb("w2_lo", [P, NE, HB * D], F32R)
        b1_s = sb("b1_s", [P, NE, 2, HB])
        b2_s = sb("b2_s", [NE, D])
        ones = sb("ones", [1, P])
        st = sb("st", [P, 2, BG, 6])
        mv = sb("mv", [P, 3, B, BG, 2])
        nrm = sb("nrm", [P, 3, B, 6, BG])
        half = sb("half", [P, 2 * BG])
        a2 = sb("a2", [P, 3, C1])
        S2 = sb("S2", [P, 4, C1])
        a3 = sb("a3", [P, 3, C2])
        S3 = sb("S3", [P, 2, C2])
        tT_hi = sb("tT_hi", [P, NU * UT], F32R)
        tT_lo = sb("tT_lo", [P, NU * UT], F32R)
        pw_hi = sb("pw_hi", [P, 2, HB, UT], F32R)
        pw_lo = sb("pw_lo", [P, 2, HB, UT], F32R)
        NT = NU * BG
        NQ = NT // 2
        m12 = sb("m12", [P, 6, NT])
        wT = sb("wT", [NE, NU * UT])
        wb_more = sb("wb_more", [P, 2, UT])

        au = sb("au", [P, 2, NG, T])
        pr = sb("pr", [P, 2, 2, L * C1])
        acuc = sb("acuc", [P, 5, L, C1])
        xnT = sb("xnT", [P, 2, T])
        Z = sb("Z", [P, 2, BG, D])
        tT = sb("tT", [P, 2, UT])
        wab_s = sb("wab_s", [P, 2, 512])

        def part(tensor, start, *shape):
            names = "abcd"[:len(tensor.shape) - 1]
            flat = tensor[:].rearrange(f"p {' '.join(names)} -> p ({' '.join(names)})")
            names = "abcd"[:len(shape)]
            return flat[:, start:start + int(np.prod(shape))].rearrange(
                f"p ({' '.join(names)}) -> p {' '.join(names)}", **dict(zip(names, shape)))

        w1_st = part(R, 0, NE, 2 * HB * P)
        w2_st = part(acuc, 0, NE, HB * D)
        wab_in = part(a2, 0, 2, NS)
        wab_pair = part(wab_s, 0, 2, P)
        acol, ucol = acuc[:, 0:3, :, :], acuc[:, 3:5, :, :]
        sq, gt = pr[:, 0, :, :], pr[:, 1, 0, :]
        S = part(au, 0, 4, L, C1)
        areal = part(wab_s, 0, 2, T)[0:B]
        ureal = part(Z, 0, 2, T)[0:B]
        hreal = xnT[0:B, :, :]
        hT = part(acuc, 0, NG, T)
        st_y = part(S2, 0, 2, BG, 6)
        TE = NT * NE
        lg = part(idft_s, 0, 2, NT, NE)
        oh = part(acuc, 2 * HB * UT, 2, NT, NE)
        eq = part(xnT, 0, NT, NE)
        wtok = part(xnT, TE, NT, NE)
        wts = part(xnT, 2 * TE, NT, NE)
        gact = au
        lin = part(acuc, 0, 2, HB, UT)
        prod = pr
        pw = [part(Z, 0, HB, UT), part(wab_s, 0, HB, UT)]
        wb = [part(dft_s, 0, UT), part(dftg, 0, UT), wb_more[:, 0, :], wb_more[:, 1, :]]
        NWB = len(wb)
        yT = part(xnT, 0, UT)
        O = part(tT, 0, BG, D)
        fin = part(tT, UT, BG, D)

        x_in = [sem(f"x_in{b}") for b in range(B)]
        first_in = sem("first_in")
        small_in = sem("small_in")
        dft_in = sem("dft_in")
        w1_in = sem("w1_in")
        w2_in = sem("w2_in")
        w1_round = sem("w1_round")
        w2_round = sem("w2_round")
        w1_split = sem("w1_split")
        w2_split = sem("w2_split")
        setup = sem("setup")
        wab_zero = sem("wab_zero")
        wab_done = sem("wab_done")
        gam_sig = sem("gam_sig")
        gam_scaled = sem("gam_scaled")
        half_set = sem("half_set")
        dve_chain = sem("dve_chain")
        pool_chain = sem("pool_chain")
        x_stats = sem("x_stats")
        x_scales = sem("x_scales")
        z_done = sem("z_done")
        zT_done = sem("zT_done")
        xn_done = sem("xn_done")
        proj_done = sem("proj_done")
        r0_done = sem("r0_done")
        skip_done = sem("skip_done")
        a_done = sem("a_done")
        u_done = sem("u_done")
        ahat_done = sem("ahat_done")
        ahat_read = sem("ahat_read")
        uhat_done = sem("uhat_done")
        sq_done = sem("sq_done")
        mag2_done = sem("mag2_done")
        mag_done = sem("mag_done")
        abs_done = sem("abs_done")
        areal_done = sem("areal_done")
        guard_done = sem("guard_done")
        gate_done = sem("gate_done")
        ucol_done = sem("ucol_done")
        scan_done = sem("scan_done")
        ih_done = sem("ih_done")
        hT_done = sem("hT_done")
        y_done = sem("y_done")
        y_stats = sem("y_stats")
        y_scales = sem("y_scales")
        yn_done = sem("yn_done")
        x1_done = sem("x1_done")
        x1_stats = sem("x1_stats")
        x1_scales = sem("x1_scales")
        t_done = sem("t_done")
        tTr_done = sem("tTr_done")
        tT_done = sem("tT_done")
        tT_split = sem("tT_split")
        r1_done = sem("r1_done")
        logit_done = sem("logit_done")
        logit_read = sem("logit_read")
        gap_done = sem("gap_done")
        prob_done = sem("prob_done")
        wts_done = sem("wts_done")
        wTr_done = sem("wTr_done")
        wT_done = sem("wT_done")
        gl_ready = sem("gl_ready")
        g_done = sem("g_done")
        l_done = sem("l_done")
        silu_done = sem("silu_done")
        weights_out = [sem(f"weights_out{k}") for k in range(NU)]
        wb_in = [sem(f"wb_in{k}") for k in range(NWB)]
        p_done = sem("p_done")
        hi_done = sem("hi_done")
        lo0_done = sem("lo0_done")
        lo1_done = sem("lo1_done")
        pw_done = sem("pw_done")
        y2_done = sem("y2_done")
        yT_done = sem("yT_done")
        tr_done = sem("tr_done")
        clip_done = sem("clip_done")
        o_done = sem("o_done")
        o_bn = sem("o_bn")
        o_stats = sem("o_stats")
        o_pow = sem("o_pow")
        o_neg = sem("o_neg")
        o_scale = sem("o_scale")
        on_done = sem("on_done")
        fin_done = sem("fin_done")
        fin_free = sem("fin_free")
        out_done = sem("out_done")
        last_yT = sem("last_yT")
        last_tr = sem("last_tr")
        last_o = sem("last_o")
        last_bn = sem("last_bn")
        last_aggr = sem("last_aggr")
        last_stats = sem("last_stats")
        last_pow = sem("last_pow")
        last_scale = sem("last_scale")
        last_norm0 = sem("last_norm0")
        last_norm1 = sem("last_norm1")
        last_fin = sem("last_fin")

        block = ctx.enter_context(nc.Block())
        NFIRST, NSMALL = 5, 8
        NPE = 4

        def zT_bank(n):
            return bank[:, n % 2, :]

        PAIR_BANK, AHAT, UHAT, HT_BANK = 2, 6, 2, 0
        HALF = P // 2
        Y_BANKS, LOGITS = 4, 2
        Y2, TR = 4, 7

        def gl_bank(e, h):
            return (0, 5)[e % 2] if h == 0 else 2

        def tile_of(b, j):
            return (b // BG) * TT + j, b % BG

        HT2 = BG // 2
        TT_BITS = TT.bit_length() - 1

        def half_of(q):
            return slice(q * HT2, (q + 1) * HT2)

        out_v = out.rearrange("(g i) (j p) d -> p g j i d", g=NG, p=P)

        @block.sync
        def _(sp):
            for b in range(B):
                g, i = divmod(b, BG)
                sp.dma_start(X[:, g * TT:(g + 1) * TT, i, :],
                             x[b].rearrange("(j p) d -> p j d", p=P)).then_inc(x_in[b], 16)
            rest = [(rows_s[:], rows2.rearrange("(o r) d -> o r d", o=1).to_broadcast([P, 2, D])),
                    (b1_s[:], b1), (b2_s[:], b2),
                    (idft_s[:], idft), (wc4_s[:], wc4), (gate_ws[:], gate_w),
                    (gate_bs[:], gate_b.to_broadcast([P, NE])), (rank_s[:], rank)]
            assert len(rest) == NSMALL
            sp.dma_start(dft_s[:], dft).then_inc(dft_in, 16)
            sp.dma_start(w2_st, w2).then_inc(w2_in, 16)
            for dst, src in rest:
                sp.dma_start(dst, src).then_inc(small_in, 16)
            for n in range(0, NE, 4):
                sp.dma_start(w1_st[:, n:n + 4, :], w1[:, n:n + 4, :]).then_inc(w1_in, 16)

            def weights_to_dram(n):
                sp.wait_ge(wT_done, n + 1)
                sp.dma_start(token_weights[n], wT[:, n * UT:(n + 1) * UT]).then_inc(weights_out[n], 16)

            def spread_weights(u, e, reused):
                if reused:
                    sp.wait_ge(pw_done, HB * (u * NE + e - NWB + 1))
                sp.dma_start(wb[e % NWB], token_weights[bass.ds(u, 1), e, :].to_broadcast([P, UT]))\
                  .then_inc(wb_in[e % NWB], 16)

            sp.sem_inc(fin_free)
            weights_to_dram(0)
            sp.wait_ge(weights_out[0], 16)
            for e in range(NE):
                spread_weights(0, e, e >= NWB)
                if 1 <= e < NE:
                    weights_to_dram(e)
            for n in range(1, NU):
                sp.wait_ge(weights_out[n], 16)
            for e in range(NE):
                spread_weights(1, e, True)
            with sp.Fori(2, NU) as u:
                for e in range(NE):
                    spread_weights(u, e, True)
                    if e == 1:
                        sp.wait_ge(fin_done, u - 1)
                        v = u - 2
                        sp.dma_start(out_v[:, (v >> TT_BITS) & (NG - 1), v & (TT - 1), :, :], fin[:]).then_inc(out_done, 16)
                    if e == 3:
                        sp.wait_ge(out_done, 16 * (u - 1))
                        sp.sem_inc(fin_free)
            sp.wait_ge(fin_done, NU - 1)
            sp.dma_start(out_v[:, (NU - 2) // TT, (NU - 2) % TT, :, :], fin[:]).then_inc(out_done, 16)
            sp.wait_ge(out_done, 16 * (NU - 1))
            sp.sem_inc(fin_free)
            for q in range(2):
                sp.wait_ge(last_fin, q + 1)
                sp.dma_start(out_v[:, NG - 1, TT - 1, half_of(q), :],
                             fin[:, half_of(q), :]).then_inc(out_done, 16)
            sp.wait_ge(out_done, 16 * (NU + 1))

        @block.gpsimd
        def _(pool):
            chain = [0]

            def link(ins):
                chain[0] += 1
                ins.then_inc(pool_chain, 1)
                pool.wait_ge(pool_chain, chain[0])

            def loose(ins):
                chain[0] += 1
                ins.then_inc(pool_chain, 1)

            pool.memset(half[:], -0.5).then_inc(half_set, 1)
            pool.wait_ge(half_set, 1)
            pool.memset(wab_pair, 0.0).then_inc(wab_zero, 1)
            pool.wait_ge(wab_zero, 1)

            def scales(which, n, counted, done):
                v, m = nrm[:, which, n, :, :], mv[:, which, n, :, :]
                k = 1 if which == 1 else 2
                if which == 0:
                    pool.wait_ge(counted, 3 * (n + 1))
                else:
                    pool.wait_ge(counted, BG * (n + 1))
                    loose(pool.tensor_scalar(v[:, 4, :], m[:, :, 0], -1.0, None, ALU.mult))
                    if k == 2:
                        loose(pool.tensor_scalar(v[:, 1, :], m[:, :, 1], 1.0 + EPS, EPS * EPS,
                                                 ALU.mult, ALU.add))
                    link(pool.tensor_scalar(v[:, 0, :], m[:, :, 1], EPS, None, ALU.add))
                link(pool.tensor_tensor(v[:, 2:2 + k, :], v[:, 0:k, :],
                                        half[:].rearrange("p (a b) -> p a b", a=2)[:, 0:k, :], ALU.pow))
                pool.tensor_tensor(v[:, 5, :], v[:, 4, :], v[:, 2, :], ALU.mult).then_inc(done, 1)

            def skip_term(u):
                r = R[:, u, :, :]
                pool.wait_ge(r0_done, BG * (u + 1))
                ins = pool.tensor_tensor(r, r, rows_s[:, 0:1, :].to_broadcast([P, BG, D]), ALU.mult)
                if u >= NPE:
                    link(ins)
                    ins = pool.tensor_tensor(r, r, rows_s[:, 1:2, :].to_broadcast([P, BG, D]), ALU.add)
                ins.then_inc(skip_done, 1)

            def weight_rest(n, rounded, hi, lo, source, done):
                pool.wait_ge(rounded, n + 1)
                pool.tensor_tensor(lo[:, n, :], source[:, n, :], hi[:, n, :].bitcast(F32),
                                   ALU.subtract).then_inc(done, 1)

            for b in range(B):
                scales(0, b, x_stats, x_scales)
                if b == 1:
                    pool.wait_ge(first_in, 16 * NFIRST)
                    for i in range(2):
                        pool.tensor_copy(wab_pair[:, i, :].rearrange("p (r i n) -> p r i n", r=2, n=NS)[:, :, i, :],
                                         wab_in).then_inc(wab_done, 1)
                if b == 3:
                    pool.wait_ge(gam_sig, 1)
                    pool.wait_ge(dft_in, 16)
                    pool.tensor_scalar(dftg[:], dft_s[:], gam[:, 1:2], None, ALU.mult).then_inc(gam_scaled, 1)
            for n in range(NE):
                weight_rest(n, w2_round, w2_hi, w2_lo, w2_st, w2_split)
            pool.wait_ge(small_in, 16 * NSMALL)
            pool.tensor_scalar(b1_s[:, :, 1, :], b1_s[:, :, 1, :], 1.0, None, ALU.add).then_inc(setup, 1)
            pool.tensor_scalar(b2_s[:], b2_s[:], ALPHA, None, ALU.mult).then_inc(setup, 1)
            pool.memset(ones[:], 1.0).then_inc(setup, 1)
            for n in range(NE):
                weight_rest(n, w1_round, w1_hi, w1_lo, w1_st, w1_split)
                if n >= 2:
                    skip_term(n - 2)
            for n in range(NE - 2, NE):
                skip_term(n)

            for n in range(NU + 1):
                if n < NU:
                    scales(1, n, y_stats, y_scales)
                if n >= 1:
                    scales(2, n - 1, x1_stats, x1_scales)

            def weigh(u, s, e, reused):
                pool.wait_ge(p_done, s + 1)
                pool.wait_ge(wb_in[e % NWB], 16 * (NE // NWB * u + e // NWB + 1))
                if reused:
                    pool.wait_ge(lo0_done, s - 1)
                    pool.wait_ge(lo1_done, s - 1)
                for h in range(HB):
                    pool.tensor_tensor(pw[e % 2][:, h, :], prod[:, e % 2, h, :], wb[e % NWB],
                                       ALU.mult).then_inc(pw_done, 1)

            def low_half(s, e):
                pool.wait_ge(hi_done, s * 2 + 1)
                pool.tensor_tensor(pw_lo[:, e % 2, 0, :], pw[e % 2][:, 0, :],
                                   pw_hi[:, e % 2, 0, :].bitcast(F32), ALU.subtract).then_inc(lo0_done, 1)

            def out_scale(v):
                pool.wait_ge(o_stats, v + 1)
                w = nrm[:, 0, 0, :, :]
                pool.tensor_tensor(w[:, 2, :], w[:, 0, :], half[:, 0:BG], ALU.pow).then_inc(o_pow, 1)
                pool.wait_ge(o_pow, v + 1)
                pool.tensor_tensor(w[:, 5, :], w[:, 4, :], w[:, 2, :], ALU.mult).then_inc(o_scale, 1)

            def group(u, first, last):
                for e in range(NE):
                    s = u * NE + e
                    if not (last and e == NE - 1):
                        weigh(u, s, e, not (first and e < 2))
                        low_half(s, e)
                    if not first and e == 4:
                        out_scale(u - 1)

            group(0, True, False)
            with pool.Fori(1, NU - 1) as u:
                group(u, False, False)
            group(NU - 1, False, True)
            for q in range(2):
                pool.wait_ge(last_stats, 2 * (q + 1))
                w = nrm[:, 0, 1 + q, :, 0:HT2]
                pool.tensor_tensor(w[:, 2, :], w[:, 0, :], half[:, 0:HT2], ALU.pow).then_inc(last_pow, 1)
                pool.wait_ge(last_pow, q + 1)
                pool.tensor_tensor(w[:, 5, :], w[:, 4, :], w[:, 2, :], ALU.mult).then_inc(last_scale, 1)

        @block.scalar
        def _(act):
            first = [(ident_s[:], ident), (cols_s[:], cols3), (wab_in, wab), (bab_s[:], bab),
                     (gam[:, 0:1], log_gamma.to_broadcast([P, 1]))]
            assert len(first) == NFIRST
            for dst, src in first:
                act.dma_start(dst, src).then_inc(first_in, 16)

            def normal_x(u):
                g, j = divmod(u, TT)
                act.wait_ge(w1_split, u + 1)
                for i in range(BG):
                    b = g * BG + i
                    act.activation(R[:, u, i, :], X[:, u, i, :], ACT.Identity,
                                   bias=nrm[:, 0, b, 5, j:j + 1],
                                   scale=nrm[:, 0, b, 2, j:j + 1]).then_inc(r0_done, 1)

            def round_weights(n, hi, source, rounded):
                act.activation(hi[:, n, :], source[:, n, :], ACT.Identity).then_inc(rounded, 1)

            EARLY = 3

            def round_w1(start, end):
                for n in range(start, end):
                    round_weights(n, w1_hi, w1_st, w1_round)

            def split_pair(p):
                g, rows = p // 2, slice(HALF * (p % 2), HALF * (p % 2) + HALF)
                act.wait_ge(proj_done, 2 * (p + 1))
                act.activation(au[rows, 0, g, :], bank[0:HALF, PAIR_BANK + p, :], ACT.Tanh,
                               bias=bab_s[0:HALF, 0:1]).then_inc(a_done, 1)
                act.activation(au[rows, 1, g, :], bank[HALF:P, PAIR_BANK + p, :], ACT.Identity,
                               bias=bab_s[HALF:P, 1:2]).then_inc(u_done, 1)

            def turn_x(b):
                act.wait_ge(zT_done, b + 1)
                if b >= 2:
                    act.wait_ge(proj_done, b - 1)
                act.activation(xnT[:, b % 2, :], zT_bank(b), ACT.Identity, bias=cols_s[:, 1:2],
                               scale=cols_s[:, 0:1]).then_inc(xn_done, 1)

            act.wait_ge(first_in, 16 * NFIRST)
            act.activation(gam[:, 1:2], gam[:, 0:1], ACT.Sigmoid).then_inc(gam_sig, 1)
            for b in range(B + 1):
                if b >= 1:
                    turn_x(b - 1)
                if b == B:
                    act.wait_ge(w1_in, 32)
                    round_w1(0, EARLY)
                if b >= 3 and b % 2 == 1 or b == B:
                    split_pair((b - 2) // 2)
                if B - 3 <= b < B:
                    act.wait_ge(w2_in, 16)
                    for n in range(3 * (b - B + 3), min(3 * (b - B + 3) + 3, NE)):
                        round_weights(n, w2_hi, w2_st, w2_round)
            act.activation(gam[:, 0:1], half[:, 0:1], ACT.Sqrt, scale=-1.0).then_inc(mag_done, 1)
            round_w1(EARLY, NE - 2)
            act.wait_ge(ahat_done, 1)
            act.activation(sq[:], bank[:, AHAT:AHAT + 2, :], ACT.Square).then_inc(sq_done, 1)
            act.activation(areal[:], bank[0:B, AHAT:AHAT + 2, :], ACT.Abs).then_inc(abs_done, 1)
            act.wait_ge(guard_done, 1)
            act.activation(gt[:], gt[:], ACT.Sqrt).then_inc(mag_done, 1)
            act.wait_ge(mag_done, 2)
            act.activation(gt[:], gt[:], ACT.Sigmoid, bias=2.0, scale=-2.0).then_inc(gate_done, 1)
            act.wait_ge(uhat_done, 1)
            act.wait_ge(w2_split, NE)
            act.activation(ucol[:], bank[:, UHAT:UHAT + 2, :].rearrange("p r (c l) -> p r l c", l=L),
                           ACT.Identity).then_inc(ucol_done, 1)
            act.wait_ge(guard_done, 2)
            act.activation(areal[:], areal[:], ACT.Sigmoid, bias=2.0, scale=-2.0).then_inc(areal_done, 1)
            act.activation(ureal[:], bank[0:B, UHAT:UHAT + 2, :], ACT.Identity).then_inc(areal_done, 1)

            for n in range(NU):
                normal_x(n)
                if n == 0:
                    round_w1(NE - 2, NE)

            def time_order(n):
                g, j = divmod(n, TT)
                act.wait_ge(ih_done, n + 1)
                act.activation(hT[:, g, j * P:(j + 1) * P].rearrange("p (c l) -> p l c", l=L),
                               bank[:, HT_BANK + n % 2, 0:P].rearrange("p (l c) -> p l c", l=L),
                               ACT.Identity).then_inc(hT_done, 1)

            for n in range(4):
                time_order(n)

            def route_probs(q):
                tl = slice(q * NQ, (q + 1) * NQ)
                act.wait_ge(gap_done, 2 * (q + 1))
                act.activation(m12[:, 4:6, tl], m12[:, 2:4, tl], ACT.Sigmoid).then_inc(prob_done, 1)

            for n in range(NU + 3):
                if n == NU + 2:
                    route_probs(0)
                if n < NU:
                    act.wait_ge(y_scales, n + 1)
                    for i in range(BG):
                        act.activation(R[:, n, i, :], bank[:, Y_BANKS + n % 4, i * D:(i + 1) * D],
                                       ACT.Identity, bias=nrm[:, 1, n, 5, i:i + 1],
                                       scale=nrm[:, 1, n, 2, i:i + 1]).then_inc(yn_done, 1)
                if n == 1:
                    for m in range(4, NU):
                        time_order(m)
                if 3 <= n < NU + 3:
                    m = n - 3
                    act.wait_ge(tTr_done, m + 1)
                    if m >= 2:
                        act.wait_ge(tT_split, m - 1)
                        act.wait_ge(logit_done, m - 1)
                    act.activation(tT[:, m % 2, :], zT_bank(m), ACT.Identity,
                                   scale=cols_s[:, 2:3]).then_inc(tT_done, 1)
                    act.activation(tT_hi[:, m * UT:(m + 1) * UT], zT_bank(m), ACT.Identity,
                                   scale=cols_s[:, 2:3]).then_inc(tT_done, 1)
                if 3 <= n < NU + 3:
                    m = n - 3
                    act.wait_ge(x1_scales, m + 1)
                    for i in range(BG):
                        act.activation(R[:, m, i, :], X[:, m, i, :], ACT.Identity,
                                       bias=nrm[:, 2, m, 5, i:i + 1],
                                       scale=nrm[:, 2, m, 2, i:i + 1]).then_inc(r1_done, 1)

            def weights_in(n):
                act.wait_ge(wTr_done, n + 1)
                act.activation(wT[:, n * UT:(n + 1) * UT], bank[0:NE, TR, :],
                               ACT.Identity).then_inc(wT_done, 1)

            weights_in(0)

            def linear_half(s, e, h, first):
                k = s * 2 + h
                act.wait_ge(gl_ready, k + 1)
                if h == 0 and not (first and e < 2):
                    act.wait_ge(p_done, s - 1)
                act.activation(lin[:, e % 2, h, :], bank[:, gl_bank(e, h) + 1, :], ACT.Identity,
                               bias=b1_s[:, e, 1, h:h + 1]).then_inc(l_done, 1)

            def high_half(s, e, h, reused):
                act.wait_ge(pw_done, s * 2 + h + 1)
                if reused and h == 0:
                    act.wait_ge(y2_done, s - 1)
                act.activation(pw_hi[:, e % 2, h, :], pw[e % 2][:, h, :], ACT.Identity).then_inc(hi_done, 1)

            def evacuate_y(v):
                act.wait_ge(y2_done, (v + 1) * NE)
                act.activation(yT[:], bank[:, Y2, :], ACT.Identity).then_inc(yT_done, 1)

            def out_norm(v, tiles):
                act.wait_ge(o_scale, v + 1)
                for i in tiles:
                    act.activation(O[:, i, :], O[:, i, :], ACT.Identity, bias=nrm[:, 0, 0, 5, i:i + 1],
                                   scale=nrm[:, 0, 0, 2, i:i + 1]).then_inc(on_done, 1)

            def group(u, first):
                for e in range(NE):
                    s = u * NE + e
                    if e == 3 and not first:
                        evacuate_y(u - 1)
                    linear_half(s, e, 0, first)
                    if not (first and e < 2):
                        high_half(s - 2, (e - 2) % NE, 1, not (first and e < 4))
                    linear_half(s, e, 1, first)
                    if first and e == 0:
                        route_probs(1)
                    act.wait_ge(g_done, s * 2 + 2)
                    act.activation(gact[:, e % 2, :, :], gact[:, e % 2, :, :], ACT.Silu,
                                   scale=ALPHA).then_inc(silu_done, 1)
                    if not (first and e == 0):
                        high_half(s - 1, (e - 1) % NE, 0, not (first and e < 3))
                    if first and e < NU - 1:
                        weights_in(e + 1)
                    if not first and e == 6:
                        out_norm(u - 1, range(BG))

            group(0, True)
            with act.Fori(1, NU) as u:
                group(u, False)
            high_half(NU * NE - 2, NE - 2, 1, True)
            high_half(NU * NE - 1, NE - 1, 0, True)
            high_half(NU * NE - 1, NE - 1, 1, True)
            act.wait_ge(y2_done, NU * NE)
            for q in range(2):
                cols = slice(q * HT2 * P, (q + 1) * HT2 * P)
                act.activation(yT[:, cols], bank[:, Y2, cols], ACT.Identity).then_inc(last_yT, 1)
            for q in range(2):
                act.wait_ge(last_scale, q + 1)
                act.activation(O[:, q * HT2, :], O[:, q * HT2, :], ACT.Identity,
                               bias=nrm[:, 0, 1 + q, 5, 0:1],
                               scale=nrm[:, 0, 1 + q, 2, 0:1]).then_inc(last_norm0, 1)

        @block.vector
        def _(dve):
            chain = [0]

            def link(ins):
                chain[0] += 1
                ins.then_inc(dve_chain, 1)
                dve.wait_ge(dve_chain, chain[0])

            def loose(ins):
                chain[0] += 1
                ins.then_inc(dve_chain, 1)
                return chain[0]

            def stats(tiles, which, n, done):
                part_st = (st_y if which == 1 else st)[:, n % 2, :, :]
                if n >= 2:
                    dve.wait_ge(done, (3 if which == 0 else BG) * (n - 1))
                last = [loose(dve.bn_stats(part_st[:, k, :], tl)) for k, tl in enumerate(tiles)]
                for k in range(BG):
                    dve.wait_ge(dve_chain, last[k])
                    ins = dve.bn_aggr(mv[:, which, n, k, :], part_st[:, k, :])
                    if which == 0:
                        end = loose(ins)
                    else:
                        ins.then_inc(done, 1)
                if which == 0:
                    dve.wait_ge(dve_chain, end)
                    v, m = nrm[:, 0, n, :, :], mv[:, 0, n, :, :]
                    for ins in (dve.tensor_scalar(v[:, 0, :], m[:, :, 1], EPS, None, ALU.add),
                                dve.tensor_scalar(v[:, 1, :], m[:, :, 1], 1.0 + EPS, EPS * EPS,
                                                  ALU.mult, ALU.add),
                                dve.tensor_scalar(v[:, 4, :], m[:, :, 0], -1.0, None, ALU.mult)):
                        ins.then_inc(done, 1)

            def scaled(dst, src, which, n, k, col, done):
                dve.tensor_scalar(dst, src, mv[:, which, n, k, 0:1], nrm[:, which, n, col, k:k + 1],
                                  ALU.subtract, ALU.mult).then_inc(done, 1)

            for b in range(B + 1):
                if b < B:
                    dve.wait_ge(x_in[b], 16)
                    stats([X[:, tile_of(b, j)[0], b % BG, :] for j in range(TT)], 0, b, x_stats)
                if b >= 1:
                    a = b - 1
                    dve.wait_ge(x_scales, a + 1)
                    if a >= 2:
                        dve.wait_ge(zT_done, a - 1)
                    for j in range(TT):
                        scaled(Z[:, a % 2, j, :], X[:, tile_of(a, j)[0], a % BG, :], 0, a, j, 3, z_done)

            dve.wait_ge(sq_done, 1)
            dve.tensor_tensor(gt[:], sq[:, 0, :], sq[:, 1, :], ALU.add).then_inc(mag2_done, 1)
            dve.wait_ge(mag2_done, 1)
            dve.tensor_scalar(gt[:], gt[:], 1e-16, None, ALU.max).then_inc(guard_done, 1)
            dve.wait_ge(abs_done, 1)
            dve.tensor_scalar(areal[:], areal[:], 1e-8, None, ALU.max).then_inc(guard_done, 1)
            dve.wait_ge(gate_done, 1)
            dve.wait_ge(w2_split, NE)

            def chunked(ap):
                return ap.rearrange("p (c l) -> p l c", l=L)

            are, aim = bank[:, AHAT, :], bank[:, AHAT + 1, :]
            loose(dve.tensor_tensor(acol[:, 0, :, :], chunked(are), chunked(gt[:]), ALU.mult))
            link(dve.tensor_tensor(acol[:, 2, :, :], chunked(aim), chunked(gt[:]), ALU.mult))
            loose(dve.tensor_scalar(acol[:, 1, :, :], acol[:, 2, :, :], -1.0, None, ALU.mult))
            dve.wait_ge(ucol_done, 1)

            def real_bins():
                dve.wait_ge(areal_done, 2)
                dve.tensor_tensor(areal[:], bank[0:B, AHAT:AHAT + 2, :], areal[:],
                                  ALU.mult).then_inc(ahat_read, 1)
                dve.wait_ge(ahat_read, 1)
                for r in range(2):
                    loose(dve.tensor_tensor_scan(hreal[:, r, :], areal[:, r, :], ureal[:, r, :], 0.0,
                                                 ALU.mult, ALU.add))

            def scan_level(a, u, s, steps, width, planes):
                ks = planes // 2
                loose(dve.tensor_copy(s(0)[:, 0:2, :], u(0)))
                if ks == 2:
                    loose(dve.tensor_copy(s(0)[:, 2:3, :], a(0)[:, 0:1, :]))
                    loose(dve.tensor_copy(s(0)[:, 3:4, :], a(0)[:, 2:3, :]))
                for l in range(1, steps):
                    p1 = pr[:, 0, :, :].rearrange("p a b -> p (a b)")[:, 0:planes * width]
                    p2 = pr[:, 1, :, :].rearrange("p a b -> p (a b)")[:, 0:planes * width]
                    v1 = p1.rearrange("p (k w) -> p k w", k=planes)
                    v2 = p2.rearrange("p (k w) -> p k w", k=planes)
                    dve.wait_ge(dve_chain, chain[0])
                    loose(dve.tensor_tensor(v1, a(l)[:, 0:1, :].to_broadcast([P, planes, width]),
                                            s(l - 1), ALU.mult))
                    end = loose(dve.tensor_tensor(
                        v2.rearrange("p (k j) w -> p k j w", j=2),
                        a(l)[:, 1:3, :].rearrange("p (o j) w -> p o j w", o=1).to_broadcast([P, ks, 2, width]),
                        s(l - 1).rearrange("p (k j) w -> p k j w", j=2)[:, :, ::-1, :], ALU.mult))
                    dve.wait_ge(dve_chain, end - 1)
                    loose(dve.tensor_tensor(v1[:, 0:2, :], v1[:, 0:2, :], u(l), ALU.add))
                    dve.wait_ge(dve_chain, chain[0])
                    loose(dve.tensor_tensor(s(l), v1, v2, ALU.add))
                dve.wait_ge(dve_chain, chain[0])

            def carry_level(s, carry, groups, width):
                n = groups * width
                p1 = pr[:, 0, :, 0:n].rearrange("p r (l c) -> p r l c", l=groups)
                p2 = pr[:, 1, :, 0:n].rearrange("p r (l c) -> p r l c", l=groups)
                for r in range(2):
                    bc = carry[:, r:r + 1, :].to_broadcast([P, groups, width])
                    loose(dve.tensor_tensor(p1[:, r, :, :], s[:, 2, :, :], bc, ALU.mult))
                    loose(dve.tensor_tensor(p2[:, r, :, :], s[:, 3, :, :], bc, ALU.mult))
                dve.wait_ge(dve_chain, chain[0] - 2)
                loose(dve.tensor_tensor(p1[:, 0, :, :], p1[:, 0, :, :], s[:, 0, :, :], ALU.add))
                dve.wait_ge(dve_chain, chain[0] - 1)
                loose(dve.tensor_tensor(p1[:, 1, :, :], p1[:, 1, :, :], s[:, 1, :, :], ALU.add))
                dve.wait_ge(dve_chain, chain[0] - 1)
                loose(dve.tensor_tensor(s[:, 0, :, :], p1[:, 0, :, :], p2[:, 1, :, :], ALU.subtract))
                dve.wait_ge(dve_chain, chain[0] - 1)
                loose(dve.tensor_tensor(s[:, 1, :, :], p1[:, 1, :, :], p2[:, 0, :, :], ALU.add))
                dve.wait_ge(dve_chain, chain[0])

            def ends(s, a):
                loose(dve.tensor_copy(a[:, 0:1, :], s[:, 2:3, :]))
                loose(dve.tensor_scalar(a[:, 1:2, :], s[:, 3:4, :], -1.0, None, ALU.mult))
                loose(dve.tensor_copy(a[:, 2:3, :], s[:, 3:4, :]))
                dve.wait_ge(dve_chain, chain[0])

            scan_level(lambda l: acol[:, :, l, :], lambda l: ucol[:, :, l, :], lambda l: S[:, :, l, :],
                       L, C1, 4)
            real_bins()
            ends(S[:, :, L - 1, :], a2)
            end2 = S[:, :, L - 1, :]
            scan_level(lambda l: a2[:, :, l::L], lambda l: end2[:, 0:2, l::L], lambda l: S2[:, :, l::L],
                       L, C2, 4)
            ends(S2[:, :, L - 1::L], a3)
            end3 = S2[:, :, L - 1::L]
            scan_level(lambda l: a3[:, :, l:l + 1], lambda l: end3[:, 0:2, l:l + 1],
                       lambda l: S3[:, :, l:l + 1], C2, 1, 2)
            v2 = S2[:].rearrange("p r (c l) -> p r l c", l=L)
            carry_level(v2[:, :, :, 1:], S3[:, :, 0:C2 - 1], L, C2 - 1)
            for q in range(2):
                lo, hi = q * C1 // 2, (q + 1) * C1 // 2
                first = max(lo, 1)
                carry_level(S[:, :, :, first:hi], S2[:, 0:2, first - 1:hi - 1], L, hi - first)
                dve.tensor_copy(S[0:B, 0:2, :, lo:hi],
                                hreal[:].rearrange("p r (c l) -> p r l c", l=L)[:, :, :, lo:hi])\
                   .then_inc(scan_done, 1)

            def y_stat(n):
                dve.wait_ge(y_done, n + 1)
                stats([bank[:, Y_BANKS + n % 4, i * D:(i + 1) * D] for i in range(BG)], 1, n, y_stats)

            def x1_add(n):
                dve.wait_ge(yn_done, BG * (n + 1))
                dve.tensor_tensor(X[:, n, :, :], X[:, n, :, :], R[:, n, :, :], ALU.add).then_inc(x1_done, 1)

            def x1_stat(n):
                dve.wait_ge(x1_done, n + 1)
                stats([X[:, n, i, :] for i in range(BG)], 2, n, x1_stats)

            def t_norm(n):
                dve.wait_ge(x1_scales, n + 1)
                dve.wait_ge(zT_done, B)
                if n >= 2:
                    dve.wait_ge(tTr_done, n - 1)
                for i in range(BG):
                    scaled(Z[:, n % 2, i, :], X[:, n, i, :], 2, n, i, 3, t_done)

            def t_split(n):
                dve.wait_ge(tT_done, 2 * (n + 1))
                hi, lo = tT_hi[:, n * UT:(n + 1) * UT], tT_lo[:, n * UT:(n + 1) * UT]
                dve.tensor_tensor(lo, tT[:, n % 2, :], hi.bitcast(F32), ALU.subtract).then_inc(tT_split, 1)

            def bc8(v):
                return v.rearrange("p (t o) -> p t o", o=1).to_broadcast([P, NQ, NE])

            def bct(v):
                return v.rearrange("p (o e) -> p o e", o=1).to_broadcast([P, NQ, NE])

            def tiles(q):
                return slice(q * NQ, (q + 1) * NQ)

            def route_logits(q):
                dve.wait_ge(logit_done, (q + 1) * NU // 2)
                dve.tensor_tensor(lg[:, 0, tiles(q), :],
                                  bank[:, LOGITS + q, 0:NQ * NE].rearrange("p (t e) -> p t e", e=NE),
                                  bct(gate_bs[:]), ALU.add).then_inc(logit_read, 1)
                dve.wait_ge(logit_read, q + 1)

            def route_best(q, k):
                tl = tiles(q)
                link(dve.tensor_reduce(m12[:, k, tl], lg[:, k, tl, :], AX.X, ALU.max))
                link(dve.tensor_tensor(eq[:, tl, :], lg[:, k, tl, :], bc8(m12[:, k, tl]), ALU.is_equal))
                link(dve.tensor_tensor(eq[:, tl, :], eq[:, tl, :], bct(rank_s[:]), ALU.mult))
                link(dve.tensor_reduce(m12[:, 4, tl], eq[:, tl, :], AX.X, ALU.max))
                link(dve.tensor_tensor(oh[:, k, tl, :], bct(rank_s[:]), bc8(m12[:, 4, tl]), ALU.is_equal))
                if k == 0:
                    flat = "p t e -> p (t e)"
                    link(dve.scalar_tensor_tensor(lg[:, 1, tl, :].rearrange(flat),
                                                  oh[:, 0, tl, :].rearrange(flat), -3.0e38,
                                                  lg[:, 0, tl, :].rearrange(flat), ALU.mult, ALU.add))

            def route_gap(q):
                tl = tiles(q)
                for a, b in ((0, 1), (1, 0)):
                    dve.tensor_tensor(m12[:, 2 + a, tl], m12[:, a, tl], m12[:, b, tl],
                                      ALU.subtract).then_inc(gap_done, 1)

            def route_weights(q):
                tl = tiles(q)
                dve.wait_ge(prob_done, q + 1)
                loose(dve.tensor_tensor(wtok[:, tl, :], oh[:, 0, tl, :], bc8(m12[:, 4, tl]), ALU.mult))
                link(dve.tensor_tensor(eq[:, tl, :], oh[:, 1, tl, :], bc8(m12[:, 5, tl]), ALU.mult))
                link(dve.tensor_tensor(wtok[:, tl, :], wtok[:, tl, :], eq[:, tl, :], ALU.add))
                dve.tensor_scalar(wts[:, tl, :], wtok[:, tl, :], 1.0 / ALPHA, None, ALU.mult).then_inc(wts_done, 1)

            for n in range(NU + 4):
                for lag, stage in ((0, y_stat), (1, x1_add), (1, x1_stat), (2, t_norm), (4, t_split)):
                    if 0 <= n - lag < NU:
                        stage(n - lag)
                if n == NU:
                    route_logits(0)
                    route_best(0, 0)
                if n == NU + 1:
                    route_best(0, 1)
                    route_gap(0)
                if n == NU + 2:
                    route_weights(0)
            route_logits(1)
            route_best(1, 0)
            route_best(1, 1)
            route_gap(1)

            def glu_half(s, e, h, reused):
                if reused and h == 0:
                    dve.wait_ge(p_done, s - 1)
                dve.wait_ge(gl_ready, s * 2 + h + 1)
                dve.tensor_scalar(gact[:, e % 2, h, :], bank[:, gl_bank(e, h), :], b1_s[:, e, 0, h:h + 1],
                                  LIMIT, ALU.add, ALU.min).then_inc(g_done, 1)

            def clip(s, e):
                dve.wait_ge(l_done, s * 2 + 2)
                dve.tensor_scalar(lin[:, e % 2, :, :], lin[:, e % 2, :, :], LIMIT + 1.0, 1.0 - LIMIT,
                                  ALU.min, ALU.max).then_inc(clip_done, 1)

            def combine(s, e, reused):
                dve.wait_ge(clip_done, s + 1)
                dve.wait_ge(silu_done, s + 1)
                if reused:
                    dve.wait_ge(pw_done, s * 2 - 2)
                dve.tensor_tensor(prod[:, e % 2, :, :], lin[:, e % 2, :, :], gact[:, e % 2, :, :],
                                  ALU.mult).then_inc(p_done, 1)

            def low_half(s, e):
                dve.wait_ge(hi_done, s * 2 + 2)
                dve.tensor_tensor(pw_lo[:, e % 2, 1, :], pw[e % 2][:, 1, :],
                                  pw_hi[:, e % 2, 1, :].bitcast(F32), ALU.subtract).then_inc(lo1_done, 1)

            def out_in(v):
                dve.wait_ge(tr_done, v + 1)
                dve.tensor_tensor(O[:], bank[:, TR, :].rearrange("p (i d) -> p i d", d=D),
                                  R[:, bass.ds(v, 1), :, :].rearrange("p a i d -> p (a i) d"),
                                  ALU.add).then_inc(o_done, 1)
                dve.wait_ge(o_done, v + 1)
                for i in range(BG):
                    dve.bn_stats(st[:, 0, i, :], O[:, i, :]).then_inc(o_bn, 1)

            def out_aggregate(v):
                for i in range(BG):
                    dve.bn_aggr(mv[:, 0, 0, i, :], st[:, 0, i, :]).then_inc(o_bn, 1)
                dve.wait_ge(o_bn, (v + 1) * 2 * BG)
                dve.tensor_scalar(nrm[:, 0, 0, 4, :], mv[:, 0, 0, :, 0], -1.0, None,
                                  ALU.mult).then_inc(o_neg, 1)
                dve.tensor_scalar(nrm[:, 0, 0, 0, :], mv[:, 0, 0, :, 1], EPS, None,
                                  ALU.add).then_inc(o_stats, 1)

            def out_add(v):
                dve.wait_ge(on_done, BG * (v + 1))
                dve.wait_ge(fin_free, v + 1)
                dve.tensor_tensor(fin[:], O[:], X[:, bass.ds(v, 1), :, :].rearrange("p a i d -> p (a i) d"),
                                  ALU.add).then_inc(fin_done, 1)

            def group(u, first):
                for e in range(NE):
                    s = u * NE + e
                    if not first and e == 5:
                        dve.wait_ge(o_bn, (u - 1) * 2 * BG + BG)
                    if not (first and e == 0):
                        clip(s - 1, (e - 1) % NE)
                    glu_half(s, e, 0, not (first and e < 2))
                    if not (first and e == 0):
                        combine(s - 1, (e - 1) % NE, not (first and e < 3))
                    glu_half(s, e, 1, True)
                    if first and e == 1:
                        route_weights(1)
                    if not (first and e < 2):
                        low_half(s - 2, (e - 2) % NE)
                    if not first and e == 4:
                        out_in(u - 1)
                    if not first and e == 5:
                        out_aggregate(u - 1)
                    if not first and e == 7:
                        out_add(u - 1)

            group(0, True)
            with dve.Fori(1, NU) as u:
                group(u, False)
            clip(NU * NE - 1, NE - 1)
            combine(NU * NE - 1, NE - 1, True)
            dve.wait_ge(wb_in[NWB - 1], 16 * NU * NE // NWB)
            dve.wait_ge(p_done, NU * NE)
            dve.wait_ge(pw_done, HB * (NU * NE - 1))
            dve.wait_ge(lo0_done, NU * NE - 2)
            e = (NE - 1) % 2
            for h in range(HB):
                dve.tensor_tensor(pw[e][:, h, :], prod[:, e, h, :], wb[NWB - 1], ALU.mult).then_inc(pw_done, 1)
            low_half(NU * NE - 2, NE - 2)
            dve.wait_ge(hi_done, HB * NU * NE - 1)
            dve.wait_ge(lo0_done, NU * NE - 1)
            dve.tensor_tensor(pw_lo[:, e, 0, :], pw[e][:, 0, :], pw_hi[:, e, 0, :].bitcast(F32),
                              ALU.subtract).then_inc(lo0_done, 1)
            low_half(NU * NE - 1, NE - 1)

            for q in range(2):
                dve.wait_ge(last_tr, q + 1)
                dve.tensor_tensor(O[:, half_of(q), :],
                                  bank[:, q, 0:HT2 * P].rearrange("p (i d) -> p i d", d=D),
                                  R[:, NU - 1, half_of(q), :], ALU.add).then_inc(last_o, 1)
                dve.wait_ge(last_o, q + 1)
                for i in range(HT2):
                    dve.bn_stats(st[:, 1, q * HT2 + i, :], O[:, q * HT2 + i, :]).then_inc(last_bn, 1)
                for i in range(HT2):
                    dve.wait_ge(last_bn, q * HT2 + i + 1)
                    dve.bn_aggr(mv[:, 0, 1 + q, i, :], st[:, 1, q * HT2 + i, :]).then_inc(last_aggr, 1)
                dve.wait_ge(last_aggr, (q + 1) * HT2)
                w, m = nrm[:, 0, 1 + q, :, 0:HT2], mv[:, 0, 1 + q, 0:HT2, :]
                dve.tensor_scalar(w[:, 0, :], m[:, :, 1], EPS, None, ALU.add).then_inc(last_stats, 1)
                dve.tensor_scalar(w[:, 4, :], m[:, :, 0], -1.0, None, ALU.mult).then_inc(last_stats, 1)
            dve.wait_ge(fin_free, NU)
            for q in range(2):
                dve.wait_ge(last_scale, q + 1)
                k = q * HT2 + 1
                scaled(O[:, k, :], O[:, k, :], 0, 1 + q, 1, 2, last_norm1)
                dve.wait_ge(last_norm0, q + 1)
                dve.wait_ge(last_norm1, q + 1)
                dve.tensor_tensor(fin[:, half_of(q), :], O[:, half_of(q), :], X[:, NU - 1, half_of(q), :],
                                  ALU.add).then_inc(last_fin, 1)

        @block.tensor
        def _(pe):
            pe.wait_ge(first_in, 16 * NFIRST)

            def turn_four(dst, src, done):
                for i in range(BG):
                    last = pe.transpose(dst[:, i * P:(i + 1) * P], src(i), ident_s[:])
                last.then_inc(done, 1)

            def transform(g, which=(0, 1)):
                for k in which:
                    done, to, table = ((a_done, AHAT, dftg), (u_done, UHAT, dft_s))[k]
                    pe.wait_ge(done, 2 * (g + 1))
                    for r in range(2):
                        last = pe.matmul(bank[:, to + r, :], table[:, r, g, :], au[:, k, g, :],
                                         start=(g == 0), stop=(g == NG - 1))
                    if g == NG - 1:
                        last.then_inc((ahat_done, uhat_done)[k], 1)

            for b in range(B + 1):
                if b < B:
                    pe.wait_ge(z_done, TT * (b + 1))
                    if b >= 2:
                        pe.wait_ge(xn_done, b - 1)
                    turn_four(zT_bank(b), lambda i: Z[:, b % 2, i, :], zT_done)
                if b >= 1:
                    if b == 1:
                        pe.wait_ge(wab_done, 2)
                    pe.wait_ge(xn_done, b)
                    p, i = divmod(b - 1, 2)
                    last = pe.matmul(bank[:, PAIR_BANK + p, :], wab_pair[:, i, :], xnT[:, (b - 1) % 2, :],
                                     start=(i == 0), stop=(i == 1))
                    last.then_inc(proj_done, 1)
                if b == 6:
                    pe.wait_ge(dft_in, 16)
                    pe.wait_ge(gam_scaled, 1)
                    transform(0, (0,))
                if b == 8:
                    transform(0, (1,))
            transform(1)

            def skip_in(n):
                if n >= 4:
                    pe.wait_ge(yn_done, BG * (n - 3))
                pe.wait_ge(skip_done, n + 1)
                y = bank[:, Y_BANKS + n % 4, :]
                if n < NPE:
                    pe.matmul(y, ones[:], rows_s[0:1, 1:2, :].to_broadcast([1, BG, D]), start=True, stop=False)
                pe.matmul(y, ident_s[:], R[:, n, :, :].rearrange("p i d -> p (i d)"),
                          start=(n >= NPE), stop=False)

            pe.wait_ge(setup, 3)
            pe.wait_ge(small_in, 16 * NSMALL)
            pe.wait_ge(ahat_read, 1)
            for n in range(4):
                skip_in(n)
            def inverse(n):
                g, j = divmod(n, TT)
                pe.wait_ge(scan_done, 1 + (j >= TT // 2))
                if n >= 2:
                    pe.wait_ge(hT_done, n - 1)
                cs = slice(j * C1 // TT, (j + 1) * C1 // TT)
                for r in range(2):
                    last = pe.matmul(bank[:, HT_BANK + n % 2, 0:P], idft_s[:, r, g, :], S[:, r, :, cs],
                                     start=(r == 0), stop=(r == 1))
                last.then_inc(ih_done, 1)

            def project(n):
                g, j = divmod(n, TT)
                pe.wait_ge(hT_done, n + 1)
                pe.matmul(bank[:, Y_BANKS + n % 4, :], hT[:, g, j * P:(j + 1) * P], wc4_s[:],
                          start=False, stop=True).then_inc(y_done, 1)

            def turn_t(n):
                pe.wait_ge(t_done, BG * (n + 1))
                pe.wait_ge(hT_done, NU)
                if n >= 2:
                    pe.wait_ge(tT_done, 2 * (n - 1))
                turn_four(zT_bank(n), lambda i: Z[:, n % 2, i, :], tTr_done)

            def logits(n):
                pe.wait_ge(tT_done, 2 * n + 1)
                for i in range(BG):
                    q, t = divmod(n * BG + i, NQ)
                    last = pe.matmul(bank[:, LOGITS + q, t * NE:(t + 1) * NE], tT[:, n % 2, i * P:(i + 1) * P],
                                     gate_ws[:], start=True, stop=True)
                last.then_inc(logit_done, 1)

            inverse(0)
            for n in range(4):
                inverse(n + 1)
                project(n)
            for n in range(5, NU):
                inverse(n)
            for n in range(NU + 1):
                if n + 4 < NU:
                    skip_in(n + 4)
                    project(n + 4)
                if n < NU:
                    turn_t(n)
                if n >= 1:
                    logits(n - 1)

            def turn_weights(n):
                pe.wait_ge(wts_done, n // TT + 1)
                if n >= 1:
                    pe.wait_ge(wT_done, n)
                for i in range(BG):
                    last = pe.transpose(bank[0:NE, TR, i * P:(i + 1) * P],
                                        wts[:, n * BG + i, :], ident_s[:])
                last.then_inc(wTr_done, 1)

            turn_weights(0)

            def mlp1_half(u, s, e, h, first):
                k = s * 2 + h
                if first and e == 0 and h == 1:
                    pe.wait_ge(logit_read, 2)
                if not (first and e < (2, 1)[h]):
                    pe.wait_ge(g_done, k - (3, 1)[h])
                    pe.wait_ge(l_done, k - (3, 1)[h])
                hi, lo = tT_hi[:, bass.ds(u * UT, UT)], tT_lo[:, bass.ds(u * UT, UT)]
                for r in range(2):
                    dst = bank[:, gl_bank(e, h) + r, :]
                    c = (r * HB + h) * P
                    whi_, wlo_ = w1_hi[:, e, c:c + P], w1_lo[:, e, c:c + P]
                    pe.matmul(dst, whi_, hi, start=True, stop=False)
                    pe.matmul(dst, whi_, lo, start=False, stop=False)
                    last = pe.matmul(dst, wlo_, hi, start=False, stop=True)
                last.then_inc(gl_ready, 1)

            def mlp2(u, s, e, first):
                if e == 0 and not first:
                    pe.wait_ge(yT_done, u)
                pe.wait_ge(lo0_done, s + 1)
                pe.wait_ge(lo1_done, s + 1)
                y = bank[:, Y2, :]
                for h in range(HB):
                    whi_, wlo_ = w2_hi[:, e, h * D:(h + 1) * D], w2_lo[:, e, h * D:(h + 1) * D]
                    hi, lo = pw_hi[:, e % 2, h, :], pw_lo[:, e % 2, h, :]
                    pe.matmul(y, whi_, hi, start=(e == 0 and h == 0), stop=False)
                    pe.matmul(y, whi_, lo, start=False, stop=False)
                    last = pe.matmul(y, wlo_, hi, start=False, stop=(e == NE - 1 and h == HB - 1))
                if e == 0:
                    last = pe.matmul(y, b2_s[:], wT[:, bass.ds(u * UT, UT)], start=False, stop=False)
                last.then_inc(y2_done, 1)

            def turn_y(v):
                pe.wait_ge(yT_done, v + 1)
                turn_four(bank[:, TR, :], lambda i: yT[:, i * P:(i + 1) * P], tr_done)

            def group(u, first):
                for e in range(NE):
                    s = u * NE + e
                    mlp1_half(u, s, e, 0, first)
                    mlp1_half(u, s, e, 1, first)
                    if e >= 3:
                        mlp2(u, s - 3, e - 3, first)
                    elif not first:
                        mlp2(u - 1, s - 3, e + NE - 3, False)
                    if e == 3 and not first:
                        turn_y(u - 1)
                    if first and e < NU - 1:
                        turn_weights(e + 1)

            pe.wait_ge(w1_split, NE)
            pe.wait_ge(w2_split, NE)
            pe.wait_ge(tT_done, 2 * NU)
            pe.wait_ge(tT_split, 1)
            pe.wait_ge(wT_done, 1)
            group(0, True)
            pe.wait_ge(tT_split, NU)
            with pe.Fori(1, NU) as u:
                group(u, False)
            mlp2(NU - 1, NU * NE - 3, NE - 3, False)
            mlp2(NU - 1, NU * NE - 2, NE - 2, False)
            pe.wait_ge(hi_done, HB * NU * NE)
            e = NE - 1
            for h in range(HB):
                for w in (w2_hi, w2_lo):
                    pe.matmul(bank[:, Y2, :], w[:, e, h * D:(h + 1) * D], pw_hi[:, e % 2, h, :],
                              start=False, stop=False)
            for h, done in ((0, lo0_done), (1, lo1_done)):
                pe.wait_ge(done, NU * NE)
                last = pe.matmul(bank[:, Y2, :], w2_hi[:, e, h * D:(h + 1) * D], pw_lo[:, e % 2, h, :],
                                 start=False, stop=(h == HB - 1))
            last.then_inc(y2_done, 1)
            pe.wait_ge(g_done, HB * NU * NE)
            pe.wait_ge(l_done, HB * NU * NE)
            for q in range(2):
                pe.wait_ge(last_yT, q + 1)
                for i in range(HT2):
                    k = q * HT2 + i
                    last = pe.transpose(bank[:, q, i * P:(i + 1) * P], yT[:, k * P:(k + 1) * P], ident_s[:])
                last.then_inc(last_tr, 1)


def kernel(**inputs):
    import concourse.bacc as bacc
    from concourse.bass_utils import run_bass_kernel_spmd

    a = {k.split("_", 2)[2]: np.asarray(v) for k, v in inputs.items()}
    f = a["x"].dtype
    wc4 = np.zeros((P, BG * D), f)
    for i in range(BG):
        wc4[i * NS:(i + 1) * NS, i * D:(i + 1) * D] = a["WC_w"].T
    arrays = {
        "x": a["x"],
        "wab": np.stack([a["Wa_w"].T, a["WB_w"].T], 1),
        "bab": np.stack([np.tile(a["Wa_b"], BG), np.tile(a["WB_b"], BG)], 1),
        "log_gamma": a["log_gamma"].reshape(1, 1),
        "wc4": wc4,
        "rows2": np.stack([a["D_skip"], a["WC_b"]]),
        "cols3": np.stack([a["ln_w"], a["ln_b"], a["norm_scale"]], 1),
        "gate_w": a["gate_w"],
        "gate_b": a["gate_b"].reshape(1, NE),
        "w1": a["mlp1_w"].reshape(NE, D, HB * P, 2).transpose(1, 0, 3, 2).reshape(P, NE, 2 * HB * P),
        "b1": a["mlp1_b"].reshape(NE, HB, P, 2).transpose(2, 0, 3, 1),
        "w2": a["mlp2_w"].reshape(NE, HB, P, D).transpose(2, 0, 1, 3).reshape(P, NE, HB * D),
        "b2": a["mlp2_b"],
    }
    arrays |= {k: v.astype(np.float32) for k, v in shape_constants().items()}
    order = ["x", "wab", "bab", "log_gamma", "wc4", "rows2", "cols3", "gate_w", "gate_b", "w1", "b1",
             "w2", "b2", "ident", "dft", "idft", "rank"]
    nc = bacc.Bacc("TRN2", target_bir_lowering=False, num_devices=1)
    feeds, args = {}, []
    for name in order:
        arr = np.ascontiguousarray(arrays[name])
        feeds[f"in_{name}"] = arr
        args.append(nc.dram_tensor(f"in_{name}", arr.shape, mybir.dt.from_np(arr.dtype),
                                   kind="ExternalInput").ap())
    args.append(nc.dram_tensor("out_0", (B, T, D), F32, kind="ExternalOutput").ap())
    args.append(nc.dram_tensor("token_weights", (NU, NE, UT), F32, kind="Internal").ap())
    build(nc, *args)
    r = run_bass_kernel_spmd(nc, [feeds], core_ids=[0])
    return r.results[0]["out_0"]
```
